# Optimizing a Trainium2 kernel written in Bass

```python
import numpy as np
import jax
import jax.numpy as jnp

def _softmax(x, axis=-1):
    return jax.nn.softmax(x, axis=axis)

def _gelu(x):
    return jax.nn.gelu(x, approximate=True)

def _silu(x):
    return jax.nn.silu(x)

def _sigmoid(x):
    return jax.nn.sigmoid(x)

def _layernorm(x, axis=-1, eps=1e-05):
    m = jnp.mean(x, axis=axis, keepdims=True)
    v = jnp.var(x, axis=axis, keepdims=True)
    return (x - m) / jnp.sqrt(v + eps)

def _scatter_add(tgt, idx, src, axis=0):
    return tgt.at[idx].add(src)

def _segment_sum(src, seg, n):
    return jax.ops.segment_sum(src, seg, n)
kernel_name = 'mk_adaln_d1_jaxref_r4_0a29e5'

def setup_inputs(seed: int=0):
    np.random.seed(seed)
    _w = jnp.asarray

    def _L0_attn_setup():
        import jax, jax.numpy as jnp
        import numpy as np
        B, C, L = (64, 128, 1024)
        key = jax.random.key(seed)
        x = jax.random.normal(key, (B, C, L), dtype=jnp.float32)
        return {'x': x}
    _L0_attn_in = _L0_attn_setup()

    def _L0_ffn_setup():
        import jax, jax.numpy as jnp
        import numpy as np
        D_MODEL = 1024
        D_FF = 2752
        key = jax.random.key(seed)
        k1, k2, k3, k4 = jax.random.split(key, 4)
        x = jax.random.normal(k1, (2, 512, D_MODEL), dtype=jnp.float32)
        W_gate = jax.random.normal(k2, (D_FF, D_MODEL), dtype=jnp.float32) * D_MODEL ** (-0.5)
        W_up = jax.random.normal(k3, (D_FF, D_MODEL), dtype=jnp.float32) * D_MODEL ** (-0.5)
        W_down = jax.random.normal(k4, (D_MODEL, D_FF), dtype=jnp.float32) * D_FF ** (-0.5)
        return {'x': x, 'W_gate': W_gate, 'W_up': W_up, 'W_down': W_down}
    _L0_ffn_in = _L0_ffn_setup()
    _L0_c = _w((lambda *s: np.random.randn(*s).astype(np.float32) * 0.05)(2, 1024))
    _L0_wmod = _w((lambda *s: np.random.randn(*s).astype(np.float32) * 0.05)(1024, 6 * 1024) * 1024 ** (-0.5))
    _d = {'L0_attn_x': _L0_attn_in['x'], 'L0_ffn_W_gate': _L0_ffn_in['W_gate'], 'L0_ffn_W_up': _L0_ffn_in['W_up'], 'L0_ffn_W_down': _L0_ffn_in['W_down'], 'L0_c': _L0_c, 'L0_wmod': _L0_wmod}
    _x0 = _d['L0_attn_x']
    _d['L0_attn_x'] = jax.random.normal(jax.random.fold_in(jax.random.key(seed), 1), (2, 2048, 1024), dtype=_x0.dtype)
    del _x0
    return _d

def reference(L0_attn_x, L0_ffn_W_gate, L0_ffn_W_up, L0_ffn_W_down, L0_c, L0_wmod):

    def _L0_attn_ref(x):
        import jax, jax.numpy as jnp
        import numpy as np
        B, C, L = (64, 128, 1024)
        b, c, l = x.shape
        q = jnp.transpose(x, (2, 0, 1))
        scale = jnp.asarray(c, x.dtype) ** 0.5
        scores = jnp.einsum('lnc,lmc->lnm', q, q) / scale
        prob = jax.nn.softmax(scores, axis=-1)
        msg = jnp.einsum('lnm,lmc->lnc', prob, q)
        return x + jnp.transpose(msg, (1, 2, 0))

    def _L0_ffn_ref(x, W_gate, W_up, W_down):
        import jax, jax.numpy as jnp
        import numpy as np
        D_MODEL = 1024
        D_FF = 2752
        out_shape = x.shape[:-1] + (W_down.shape[0],)
        xf = x.reshape(-1, x.shape[-1])
        up = jnp.einsum('td,fd->tf', xf, W_up)
        gate = jax.nn.silu(jnp.einsum('td,fd->tf', xf, W_gate))
        h = gate * up
        y = jnp.einsum('tf,df->td', h, W_down)
        return y.reshape(out_shape)
    x = L0_attn_x
    mod = (_silu(L0_c) @ L0_wmod).reshape(L0_c.shape[0], 6, 1, -1)
    sa, ca, ga, sb, cb, gb = (mod[:, 0], mod[:, 1], mod[:, 2], mod[:, 3], mod[:, 4], mod[:, 5])
    ga = (2 * (ga >= 0) - 1) * jnp.maximum(jnp.abs(ga), 0.25)
    gb = (2 * (gb >= 0) - 1) * jnp.maximum(jnp.abs(gb), 0.25)
    h = _layernorm(x, axis=-1) * (1 + ca) + sa
    x = x + ga * _L0_attn_ref(h)
    h = _layernorm(x, axis=-1) * (1 + cb) + sb
    x = x + gb * _L0_ffn_ref(h, L0_ffn_W_gate, L0_ffn_W_up, L0_ffn_W_down)
    return x

_drawn_inputs = setup_inputs


def setup_inputs(seed=0):
    import zlib

    import numpy as np

    out = dict(_drawn_inputs(seed))
    spreads = {}
    factors = {}
    for name, (base, spread) in spreads.items():
        noise = np.random.default_rng([zlib.crc32(name.encode()), seed]).standard_normal(out[name].shape)
        drawn = base * np.exp(spread * noise) if base else spread * noise
        out[name] = jnp.asarray(drawn.astype(out[name].dtype))
    for name, factor in factors.items():
        out[name] = (out[name] * factor).astype(out[name].dtype)
    return out
```

```python
import numpy as np

import concourse.bass as bass
from concourse import mybir
from concourse.alu_op_type import AluOpType as ALU

F32 = mybir.dt.float32
F32R = mybir.dt.float32r
ACT = mybir.ActivationFunctionType

P = 128
NB = 2
D = 1024
C = 2048
F = 2752
KD = D // P
CC = 256
T = NB * CC
NCH = C // CC
NPAIR = NCH // 2
NMOD = 6
FT = F // P
TAIL = F - FT * P
assert 2 * TAIL == P
HALF0 = (FT + 1) // 2
HALF1 = FT - HALF0
HT = HALF0
assert HALF1 + 1 == HT
GU = 2 * KD * P
GUT = KD * P
DN = HT * P
NGU = FT + 1
NDN = 2 * KD
NSLOT = NGU + NDN
P_DN0 = HALF0
P_GU1 = P_DN0 + KD
P_TAIL = P_GU1 + HALF1
P_DN1 = P_TAIL + 1
assert NSLOT == P_DN1 + KD and NSLOT % 2 == 0 and NGU % 2 == 0
WPART = 512
NPART = NMOD * D // WPART
LPP = WPART // P
SQ_RING = 4
EPS = 1e-5
GATE_MIN = 0.25
SCORE_SCALE = float(np.float32(1.0) / np.sqrt(np.float32(C)))


def build(nc, x, wgu, wgut, wdn, cT, wmod, out):
    base = (nc.sbuf_base + 63) // 64 * 64
    K = 1024

    def sb(name, shape, dt, at):
        return nc.alloc_sbuf_tensor_at(name, [P] + shape, dt, offset=base + at)

    xbuf = [sb("xbuf0", [2, KD, NB, CC], F32, 76 * K), sb("xbuf1", [2, KD, NB, CC], F32, 0)]
    dbuf = sb("dbuf", [2, KD, NB, CC], F32, 32 * K)
    x2_next = sb("x2_next", [KD, NB, CC], F32, 0)
    h_next = sb("h_next", [KD, NB, CC], F32, 16 * K)
    h_hi = sb("h_hi", [HT, T], F32R, 32 * K)
    h_lo = sb("h_lo", [HT, T], F32R, 54 * K)
    xn_hi = sb("xn_hi", [KD, T], F32R, 76 * K)
    xn_lo = sb("xn_lo", [KD, T], F32R, 92 * K)
    acc = sb("acc", [KD, NB, CC], F32, 108 * K)
    wm = [sb(f"wm{r}", [KD, WPART], F32, (124 + 16 * r) * K)  for r in range(2)]
    w_hi = [sb(f"w_hi{r}", [GU], F32R, (124 + 8 * r) * K) for r in range(2)]
    w_lo = [sb(f"w_lo{r}", [GU], F32R, (140 + 8 * r) * K) for r in range(2)]
    w_raw = [sb(f"w_raw{r}", [GU], F32, (156 + 8 * r) * K) for r in range(2)]
    sq = sb("sq", [SQ_RING, T], F32, 172 * K)
    sg = [sb(f"sg{r}", [T], F32, (172 + 2 * r) * K) for r in range(2)]
    prod = sb("prod", [T], F32, 176 * K)
    at = [180 * K]

    def small(name, shape, dt=F32):
        size = int(np.prod(shape)) * 4
        t = sb(name, shape, dt, at[0])
        at[0] += (size + 31) // 32 * 32
        return t

    presum = small("presum", [2, T])
    std = small("std", [2, T])
    rstd = small("rstd", [2, T])
    mean_row = small("mean_row", [2, T])
    junk_a = small("junk_a", [2, 2, CC])
    junk_v = small("junk_v", [2, 2, CC])
    ones = small("ones", [P])
    ct = small("ct", [KD, NB])
    silu_c = small("silu_c", [KD, NB])
    eps_t = small("eps_t", [1])
    part = [small(f"part{u}", [5, KD]) for u in range(2)]
    xs = small("xs", [5, KD])
    mod = small("mod", [NMOD, NB, KD])
    ca1 = small("ca1", [NB, KD])
    cb1 = small("cb1", [NB, KD])
    gate_a = small("gate_a", [2, NB, KD])
    gate_t = small("gate_t", [2, NB, KD])
    score = small("score", [NB, NB, KD])
    prob = small("prob", [NB, NB, KD])
    tmp = [small(f"tmp{i}", [NB, KD]) for i in range(5)]
    att = small("att", [NB, NB, KD])
    coef = small("coef", [3, NB, KD])
    pool_u, pool_v = presum[:, 0, :], presum[:, 1, :]
    pool_acc = mean_row[:, 0, :]
    pool_sq = mean_row[:, 1, :]
    stat1 = junk_a[:].rearrange("p r h c -> p r (h c)")
    mean2 = std[:, 1, :]
    std2 = std[:, 0, :]
    rstd2 = rstd[:, 0, :]

    assert base + at[0] <= nc.sbuf_usable_end, (base + at[0], nc.sbuf_usable_end)
    ps = nc.alloc_psum_tensor("ps", [P, 8, T], F32)
    ps_mean, ps_var, ps_mod = [ps[:, 0, :], ps[:, 1, :]], [ps[:, 2, :], ps[:, 3, :]], ps[:, 4, :]
    ps_gate, ps_up, ps_y = [ps[:, 0, :], ps[:, 1, :]], [ps[:, 2, :], ps[:, 3, :]], [ps[:, 4, :], ps[:, 5, :]]
    ps_mean2, ps_var2 = ps[:, 6, :], ps[:, 7, :]

    stats_dram = nc.dram_tensor("stats", [NCH, 2, T], F32, kind="Internal").ap()

    sem = nc.alloc_semaphore
    c_loaded, eps_ready, ones_ready = sem("c_loaded"), sem("eps_ready"), sem("ones_ready")
    x_loaded = [[sem(f"x_loaded{u}{h}") for h in range(2)] for u in range(2)]
    presum_ready, mean_mm, mean_row_ready = sem("presum_ready"), sem("mean_mm"), sem("mean_row_ready")
    centred, sq_ready, sq_used = sem("centred"), sem("sq_ready"), sem("sq_used")
    std_ready, rstd_ready, stats_saved = sem("std_ready"), sem("rstd_ready"), sem("stats_saved")
    xhat_ready, sqsum_done, cross_done = sem("xhat_ready"), sem("sqsum_done"), sem("cross_done")
    wm_loaded = [sem(f"wm_loaded{r}") for r in range(2)]
    silu_ready, mod_done = sem("silu_ready"), sem("mod_done")
    zeroed = sem("zeroed")
    shifted, exp_done, coef_ready = sem("shifted"), sem("exp_done"), sem("coef_ready")
    u0_ready, x20_ready, d20_ready, h20_ready = sem("u0_ready"), sem("x20_ready"), sem("d20_ready"), sem("h20_ready")
    dve_chain, pool_chain, pool_passed = sem("dve_chain"), sem("pool_chain"), sem("pool_passed")
    raw_loaded = [sem(f"raw_loaded{r}") for r in range(2)]
    hi_ready, lo_ready, slot_done = sem("hi_ready"), sem("lo_ready"), sem("slot_done")
    gu_bank_free, y_bank_free = sem("gu_bank_free"), sem("y_bank_free")
    silu_done, h_hi_done, h_ready = sem("silu_done"), sem("h_hi_done"), sem("h_ready")
    xn_hi_ready, xn_ready = sem("xn_hi_ready"), sem("xn_ready")
    next_free, next_x, next_stat = sem("next_free"), sem("next_x"), sem("next_stat")
    acc_ready, out_stored = sem("acc_ready"), sem("out_stored")
    sum2_ready, sq2_ready, stat2_mm, mean20_mm = sem("sum2_ready"), sem("sq2_ready"), sem("stat2_mm"), sem("mean20_mm")
    mean2_ready, std2_ready, rstd2_ready, h_next_ready = (
        sem("mean2_ready"), sem("std2_ready"), sem("rstd2_ready"), sem("h_next_ready"))

    def bc(ap, n):
        return ap[:, None, :].broadcast_to([P, n, T])

    def tok(ap):
        return ap.rearrange("p k b c -> p k (b c)")

    def kind_of(p):
        if p < P_DN0:
            return "gu", p, GU
        if p < P_GU1:
            return "dn", p - P_DN0, DN
        if p < P_TAIL:
            return "gu", p - KD, GU
        if p == P_TAIL:
            return "tail", FT, GUT
        return "dn", p - P_DN1 + KD, DN

    STEPS = []
    for first, end in ((0, 2), (2, P_DN0), (P_DN0, P_GU1), (P_GU1, P_TAIL), (P_TAIL, P_DN1), (P_DN1, P_DN1 + 1), (P_DN1 + 1, NSLOT)):
        n = max(0, (end - first - 2) // 2)
        if n:
            STEPS.append((first, n, 2))
        STEPS += [(p, 1, 1) for p in range(first + 2 * n, end)]

    def steps(eng, one):
        for first, n, per in STEPS:
            if n > 1:
                with eng.Fori(0, n) as i:
                    for u in range(per):
                        one(first + u, 2 * i)
            else:
                one(first, 0)

    block = nc.Block()
    with block as block:

        @block.sync
        def _(sp):
            def load_part(w):
                if w >= 2:
                    sp.wait_ge(mod_done, w - 1)
                sp.dma_start(wm[w % 2][:], wmod[w]).then_inc(wm_loaded[w % 2], 16)

            def load_pair(a):
                if a >= 2:
                    sp.wait_ge(centred, 2 * (a - 1))
                chunk = 2 * ((a + 1) % NPAIR)
                for h in range(2):
                    sp.dma_start(tok(xbuf[a % 2][:, h]), x[chunk + h].rearrange("p (k t) -> p k t", k=KD)).then_inc(
                        x_loaded[a % 2][h], 16)

            def save_stats(a):
                chunk = 2 * ((a + 1) % NPAIR)
                sp.wait_ge(mean_row_ready, 2 * (a + 1))
                sp.dma_start(stats_dram[chunk:chunk + 2, 0, :].rearrange("(o h) t -> o h t", o=1),
                             mean_row[0:1, :, :]).then_inc(stats_saved, 16)
                sp.wait_ge(rstd_ready, 2 * (a + 1))
                sp.dma_start(stats_dram[chunk:chunk + 2, 1, :].rearrange("(o h) t -> o h t", o=1),
                             rstd[0:1, :, :]).then_inc(stats_saved, 16)

            sp.dma_start(ct[:], cT).then_inc(c_loaded, 16)
            load_pair(0)
            load_part(0)
            load_part(1)
            load_pair(1)
            per_pair = NPART // NPAIR
            for a in range(NPAIR):
                for w in range(2 + per_pair * a, min(NPART, 2 + per_pair * (a + 1))):
                    load_part(w)
                save_stats(a)
                if a + 2 < NPAIR:
                    load_pair(a + 2)

            def load_slot(p, ahead, e):
                kind, n, size = kind_of(p % NSLOT)
                r = p % 2
                if not (isinstance(e, int) and e == 0 and isinstance(ahead, int) and p < 2):
                    sp.wait_ge(lo_ready, e * NSLOT + ahead + (p - 1))
                if kind == "gu":
                    src = wgu[bass.ds(ahead + n, 1), :, :]
                elif kind == "tail":
                    src = wgut[0:1, :, :]
                else:
                    src = wdn[bass.ds(ahead + n, 1), :, :]
                sp.dma_start(w_raw[r][:, 0:size], src.rearrange("o p w -> (o p) w")).then_inc(raw_loaded[r], 16)

            load_slot(0, 0, 0)
            load_slot(1, 0, 0)

            def store(p, ahead, e):
                m = p - P_DN1
                sp.wait_ge(y_bank_free, e * NDN + ahead + (2 + KD + m + 1))
                sp.dma_start(out[bass.ds(e, 1), :, bass.ds((ahead + m) * T, T)].rearrange("o p t -> (o p) t"),
                             acc[:, bass.ds(ahead + m, 1), :, :].rearrange("p o b c -> p (o b c)")).then_inc(out_stored, 16)

            def chunk(e, last):
                def one(p, ahead):
                    if not (last and p + 2 >= NSLOT):
                        load_slot(p + 2, ahead, e)
                    if p > P_DN1:
                        store(p - 1, ahead, e)
                    if p == 1 and not last:
                        sp.wait_ge(next_free, e + 1)
                        sp.dma_start(x2_next[:].rearrange("p k b c -> p (k b c)"),
                                     x[bass.ds(e + 1, 1), :, :].rearrange("o p w -> (o p) w")).then_inc(next_x, 16)
                        sp.dma_start(stat1.rearrange("p s t -> p (s t)"),
                                     stats_dram[bass.ds(e + 1, 1), :, :].rearrange("o s t -> o (s t)").broadcast_to(
                                         [P, 2 * T])).then_inc(next_stat, 16)
                steps(sp, one)
                store(NSLOT - 1, 0, e)

            sp.wait_ge(stats_saved, 32 * NPAIR)
            with sp.Fori(0, NCH - 1) as e:
                chunk(e, False)
            chunk(NCH - 1, True)
            sp.wait_ge(out_stored, 16 * KD * NCH)

        @block.gpsimd
        def _(pool):
            g = nc.gpsimd
            g.memset(ones[:], 1.0).then_inc(ones_ready, 1)

            per_half = KD - 1
            with pool.Fori(0, NPAIR // 2) as t:
                for u in range(2):
                    for h in range(2):
                        done = t * (4 * (per_half - 1)) + (2 * u + h) * (per_half - 1)
                        pool.wait_ge(x_loaded[u][h], t * 16 + 16)
                        pool.wait_ge(mean_mm, t * 4 + 2 * u)
                        xk = tok(xbuf[u][:, h])
                        for k in range(1, KD):
                            ins = g.tensor_tensor(presum[:, h, :], xk[:, 0, :] if k == 1 else presum[:, h, :], xk[:, k, :],
                                                  ALU.add)
                            if k < KD - 1:
                                ins.then_inc(pool_chain, 1)
                                pool.wait_ge(pool_chain, done + k)
                            else:
                                ins.then_inc(presum_ready, 1)

            chain0 = NPAIR * 2 * (per_half - 1)

            def chunk(e, first):
                count = [0]
                total = chunk_links

                def pause(sem_, value):
                    pool.wait_ge(sem_, value)
                    pool.sem_inc(pool_passed, 1)

                def link(ins):
                    ins.then_inc(pool_chain, 1)
                    count[0] += 1
                    pause(pool_chain, e * total + (chain0 + count[0]))

                if not first:
                    pause(out_stored, e * (16 * KD))
                    for k in range(KD):
                        ins = g.tensor_copy(tok(acc)[:, k, :], tok(x2_next)[:, k, :])
                        if k < KD - 1:
                            ins.then_inc(acc_ready, 1)
                    link(ins)
                    pool.nop().then_inc(acc_ready, 1)
                    pool.nop().then_inc(next_free, 1)
                pool.wait_ge(next_x, e * 16 + 16)
                pool.wait_ge(next_stat, e * 16 + 16)
                pool.wait_ge(xn_ready, e + 1)
                hk, xk = tok(h_next), tok(x2_next)
                for k in range(KD):
                    link(g.tensor_tensor(hk[:, k, :], xk[:, k, :], stat1[:, 0, :], ALU.subtract))
                    link(g.tensor_tensor(hk[:, k, :], hk[:, k, :], stat1[:, 1, :], ALU.mult))
                    for n in range(NB):
                        cols = slice(n * CC, (n + 1) * CC)
                        g.tensor_scalar(pool_u[:, cols], h_next[:, k, n, :], coef[:, 0, n, k:k + 1],
                                        coef[:, 2, n, k:k + 1], ALU.mult, ALU.add)
                        ins = g.tensor_scalar(pool_v[:, cols], h_next[:, k, 1 - n, :], coef[:, 1, n, k:k + 1], 0.0,
                                              ALU.mult, ALU.add)
                    link(ins)
                    link(g.tensor_tensor(pool_u, pool_u, pool_v, ALU.add))
                    link(g.tensor_tensor(xk[:, k, :], xk[:, k, :], pool_u, ALU.add))
                    if k == 0:
                        if not first:
                            pause(stat2_mm, e * 2)
                        link(g.tensor_copy(pool_acc, xk[:, 0, :]))
                    elif k < KD - 1:
                        link(g.tensor_tensor(pool_acc, pool_acc, xk[:, k, :], ALU.add))
                    else:
                        g.tensor_tensor(pool_acc, pool_acc, xk[:, k, :], ALU.add).then_inc(sum2_ready, 1)
                pool.wait_ge(mean2_ready, e + 1)
                for k in range(KD):
                    link(g.tensor_tensor(hk[:, k, :], xk[:, k, :], mean2, ALU.subtract))
                    if k == 0:
                        link(g.tensor_tensor(pool_acc, hk[:, 0, :], hk[:, 0, :], ALU.mult))
                    else:
                        link(g.tensor_tensor(pool_sq, hk[:, k, :], hk[:, k, :], ALU.mult))
                        ins = g.tensor_tensor(pool_acc, pool_acc, pool_sq, ALU.add)
                        if k < KD - 1:
                            link(ins)
                        else:
                            ins.then_inc(sq2_ready, 1)
                pool.wait_ge(rstd2_ready, e + 1)
                for k in range(KD):
                    link(g.tensor_tensor(hk[:, k, :], hk[:, k, :], rstd2, ALU.mult))
                    for n in range(NB):
                        ins = g.tensor_scalar(h_next[:, k, n, :], h_next[:, k, n, :], cb1[:, n, k:k + 1],
                                              mod[:, 3, n, k:k + 1], ALU.mult, ALU.add)
                    link(ins)
                pool.nop().then_inc(h_next_ready, 1)
                return count[0]

            chunk_links = (6 * KD - 1) + (3 * KD - 2) + 2 * KD + 1
            pool.wait_ge(coef_ready, 1)
            assert chunk(0, True) == chunk_links - 1
            chain0 -= 1
            with pool.Fori(1, NCH - 1) as e:
                n = chunk(e, False)
            assert n == chunk_links
            pool.wait_ge(out_stored, (NCH - 1) * 16 * KD)
            for k in range(KD):
                g.tensor_copy(tok(acc)[:, k, :], tok(x2_next)[:, k, :]).then_inc(acc_ready, 1)

        @block.scalar
        def _(act):
            s = nc.scalar
            act.wait_ge(c_loaded, 16)
            s.activation(silu_c[:], ct[:], ACT.Silu).then_inc(silu_ready, 1)
            act.wait_ge(eps_ready, 1)

            with act.Fori(0, NPAIR // 2) as t:
                for u in range(2):
                    for h in range(2):
                        act.wait_ge(centred, t * 4 + (2 * u + h + 1))
                        act.wait_ge(stats_saved, t * 64 + 32 * u)
                        s.mul(mean_row[0:1, h, :], ps_mean[h][0:1, :], 1.0 / D).then_inc(mean_row_ready, 1)
                        for k in range(KD):
                            n = (2 * u + h) * KD + k
                            if n >= SQ_RING:
                                act.wait_ge(sq_used, t * (4 * KD) + (n - SQ_RING + 1))
                            else:
                                act.wait_ge(sq_used, t * (4 * KD))
                            s.activation(sq[:, n % SQ_RING, :], tok(dbuf[:, h])[:, k, :], ACT.Square).then_inc(sq_ready, 1)
                    for h in range(2):
                        act.wait_ge(sq_used, t * (4 * KD) + (2 * u + h + 1) * KD)
                        s.activation(std[:, h, :], ps_var[h], ACT.Sqrt, bias=eps_t[:, 0:1], scale=1.0 / D).then_inc(
                            std_ready, 1)
                    for k in range(KD):
                        for b in range(NB):
                            act.wait_ge(xhat_ready, t * (4 * KD) + (2 * u * KD + NB * k + b + 1))
                            act.wait_ge(sqsum_done, t * (4 * KD) + max(0, 2 * u * KD + NB * k + b - 1))
                            s.activation(junk_a[:, b], dbuf[:, :, k, b, :], ACT.Square,
                                         accum_out=part[u][:, 2 + b, k:k + 1]).then_inc(sqsum_done, 1)

            act.wait_ge(shifted, 1)
            s.activation(prob[:], score[:], ACT.Exp).then_inc(exp_done, 1)

            act.wait_ge(coef_ready, 1)
            for k in range(KD):
                for n in range(NB):
                    ins = s.activation(xbuf[1][:, 1, k, n, :], dbuf[:, 0, k, n, :], ACT.Identity,
                                       bias=coef[:, 2, n, k:k + 1], scale=coef[:, 0, n, k:k + 1])
                ins.then_inc(u0_ready, 1)
            act.wait_ge(d20_ready, 1)
            for k in range(KD):
                act.wait_ge(sq_used, NCH * KD + max(0, k - SQ_RING + 1))
                s.activation(sq[:, k % SQ_RING, :], tok(dbuf[:, 1])[:, k, :], ACT.Square).then_inc(sq_ready, 1)
            act.wait_ge(sq_used, (NCH + 1) * KD)
            s.activation(std2, ps_var2, ACT.Sqrt, bias=eps_t[:, 0:1], scale=1.0 / D).then_inc(std_ready, 1)
            for k in range(KD):
                act.wait_ge(h20_ready, k + 1)
                s.copy(xn_hi[:, k, :], tok(dbuf[:, 1])[:, k, :]).then_inc(xn_hi_ready, 1)

            def split_hi(p, ahead, e):
                _, _, size = kind_of(p % NSLOT)
                r = p % 2
                act.wait_ge(raw_loaded[r], e * (8 * NSLOT) + 8 * ahead + (16 * (p // 2) + 16))
                if p >= 2:
                    act.wait_ge(slot_done, e * NSLOT + ahead + (p - 1))
                s.copy(w_hi[r][:, 0:size], w_raw[r][:, 0:size]).then_inc(hi_ready, 1)

            act.wait_ge(mod_done, NPART)
            split_hi(0, 0, 0)
            split_hi(1, 0, 0)

            def chunk(e, last):
                def one(p, ahead):
                    kind, n, _ = kind_of(p)
                    if kind != "dn":
                        rows = P if kind == "gu" else TAIL
                        act.wait_ge(slot_done, e * NSLOT + ahead + (p + 1))
                        act.wait_ge(gu_bank_free, e * NGU + ahead + (n + 1))
                        s.activation(sg[n % 2][0:rows, :], ps_gate[n % 2][0:rows, :], ACT.Silu).then_inc(silu_done, 1)
                    if not (last and p + 2 >= NSLOT):
                        split_hi(p + 2, ahead, e)
                    if p == P_GU1 - 1 and not last:
                        act.wait_ge(stat2_mm, e * 2 + 1)
                        s.mul(mean2, ps_mean2, 1.0 / D).then_inc(mean2_ready, 1)
                    if p == P_TAIL - 2 and not last:
                        act.wait_ge(stat2_mm, e * 2 + 2)
                        s.activation(std2, ps_var2, ACT.Sqrt, bias=eps_t[:, 0:1], scale=1.0 / D).then_inc(std2_ready, 1)
                    if p == P_DN1 and not last:
                        act.wait_ge(h_next_ready, e + 1)
                        for k in range(KD):
                            s.copy(xn_hi[:, k, :], tok(h_next)[:, k, :]).then_inc(xn_hi_ready, 1)
                steps(act, one)

            with act.Fori(0, NCH - 1) as e:
                chunk(e, False)
            chunk(NCH - 1, True)

        @block.vector
        def _(dve):
            v = nc.vector
            v.memset(eps_t[:], EPS).then_inc(eps_ready, 1)
            v.memset(xs[:], 0.0).then_inc(zeroed, 1)
            v.memset(part[1][:], 0.0).then_inc(zeroed, 1)
            dve.wait_ge(zeroed, 2)

            with dve.Fori(0, NPAIR // 2) as t:
                for u in range(2):
                    dve.wait_ge(sqsum_done, t * (4 * KD) + 2 * KD * u)
                    dve.wait_ge(cross_done, t * (2 * KD) + KD * u)
                    for h in range(2):
                        dve.wait_ge(mean_mm, t * 4 + (2 * u + h + 1))
                        v.scalar_tensor_tensor(tok(dbuf[:, h]), bc(ps_mean[h], KD), -1.0 / D, tok(xbuf[u][:, h]),
                                               ALU.mult, ALU.add).then_inc(centred, 1)
                    v.tensor_tensor(xs[:], xs[:], part[1 - u][:], ALU.add).then_inc(zeroed, 1)
                    for h in range(2):
                        dve.wait_ge(std_ready, t * 4 + (2 * u + h + 1))
                        dve.wait_ge(stats_saved, t * 64 + 32 * u)
                        v.reciprocal(rstd[:, h, :], std[:, h, :]).then_inc(rstd_ready, 1)
                    dve.wait_ge(rstd_ready, t * 4 + (2 * u + 2))

                    def cross(k):
                        dve.wait_ge(xhat_ready, t * (4 * KD) + (2 * u * KD + NB * (k + 1)))
                        dve.wait_ge(cross_done, t * (2 * KD) + max(0, KD * u + k - 1))
                        v.tensor_tensor_reduce(junk_v[:, k % 2], dbuf[:, :, k, 0, :], dbuf[:, :, k, 1, :], 1.0, 0.0, ALU.mult,
                                               ALU.add, accum_out=part[u][:, 4, k:k + 1]).then_inc(cross_done, 1)

                    for k in range(KD):
                        for b in range(NB):
                            v.scalar_tensor_tensor(dbuf[:, :, k, b, :], dbuf[:, :, k, b, :], 1.0,
                                                   rstd[:, :, b * CC:(b + 1) * CC], ALU.mult, ALU.mult,
                                                   accum_out=part[u][:, b, k:k + 1]).then_inc(xhat_ready, 1)
                        if k:
                            cross(k - 1)
                    cross(KD - 1)

            links = [0]

            def link(ins):
                ins.then_inc(dve_chain, 1)
                links[0] += 1
                dve.wait_ge(dve_chain, links[0])

            dve.wait_ge(mod_done, NPART)
            link(v.tensor_copy(mod[:], ps_mod[:, 0:NMOD * KD * NB].rearrange("p (i k b) -> p i b k", i=NMOD, k=KD)))
            v.tensor_scalar(ca1[:], mod[:, 1], 1.0, None, ALU.add)
            v.tensor_scalar(cb1[:], mod[:, 4], 1.0, None, ALU.add)
            for j in range(2):
                ins = v.tensor_scalar(gate_t[:, j], mod[:, 3 * j + 2], 0.0, 2.0, ALU.is_ge, ALU.mult)
            link(ins)
            link(v.tensor_scalar(gate_t[:], gate_t[:], -1.0, None, ALU.add))
            for j in range(2):
                ins = v.tensor_tensor(gate_a[:, j], mod[:, 3 * j + 2], gate_t[:, j], ALU.mult)
            link(ins)
            link(v.scalar_tensor_tensor(gate_a[:], gate_a[:], GATE_MIN, gate_t[:], ALU.max, ALU.mult))

            dve.wait_ge(sqsum_done, NPAIR * 2 * KD)
            dve.wait_ge(cross_done, NPAIR * KD)
            link(v.tensor_tensor(xs[:], xs[:], part[1][:], ALU.add))
            sa = mod[:, 0]
            w0, w1, w2, w3, w4 = (t_[:] for t_ in tmp)
            v.tensor_tensor(w0, ca1[:], xs[:, 2:4], ALU.mult)
            v.tensor_tensor(w1, sa, xs[:, 0:2], ALU.mult)
            v.tensor_tensor(w2, sa, sa, ALU.mult)
            v.tensor_tensor(w3[:, 0], ca1[:, 1], xs[:, 4], ALU.mult)
            link(v.tensor_tensor(w3[:, 1], ca1[:, 1], xs[:, 1], ALU.mult))
            v.scalar_tensor_tensor(w0, w1, 2.0, w0, ALU.mult, ALU.add)
            v.tensor_tensor(w4[:, 0], sa[:, 1], xs[:, 0], ALU.mult)
            link(v.tensor_scalar(w4[:, 1], sa[:, 1], float(C), None, ALU.mult))
            v.tensor_tensor(w0, w0, ca1[:], ALU.mult)
            link(v.tensor_tensor(w3, w3, w4, ALU.add))
            v.scalar_tensor_tensor(score[:, 0, 0], w2[:, 0], float(C), w0[:, 0], ALU.mult, ALU.add)
            v.scalar_tensor_tensor(score[:, 1, 1], w2[:, 1], float(C), w0[:, 1], ALU.mult, ALU.add)
            v.tensor_tensor(w4[:, 0], w3[:, 0], ca1[:, 0], ALU.mult)
            link(v.tensor_tensor(w4[:, 1], w3[:, 1], sa[:, 0], ALU.mult))
            v.tensor_tensor(score[:, 0, 1], w4[:, 0], w4[:, 1], ALU.add)
            link(v.tensor_tensor(score[:, 1, 0], w4[:, 0], w4[:, 1], ALU.add))
            link(v.tensor_tensor(w0, score[:, :, 0], score[:, :, 1], ALU.max))
            for m in range(NB):
                ins = v.tensor_tensor(score[:, :, m], score[:, :, m], w0, ALU.subtract)
            link(ins)
            v.tensor_scalar(score[:], score[:], SCORE_SCALE, None, ALU.mult).then_inc(shifted, 1)
            dve.wait_ge(exp_done, 1)
            link(v.tensor_tensor(w0, prob[:, :, 0], prob[:, :, 1], ALU.add))
            link(v.reciprocal(w1, w0))
            for m in range(NB):
                ins = v.tensor_tensor(prob[:, :, m], prob[:, :, m], w1, ALU.mult)
            link(ins)
            ga = gate_a[:, 0]
            for n in range(NB):
                v.scalar_tensor_tensor(att[:, n, n], prob[:, n, n], 1.0, ga[:, n], ALU.add, ALU.mult)
                ins = v.tensor_tensor(att[:, n, 1 - n], prob[:, n, 1 - n], ga[:, n], ALU.mult)
            link(ins)
            for n in range(NB):
                v.tensor_tensor(coef[:, 0, n], att[:, n, n], ca1[:, n], ALU.mult)
                v.tensor_tensor(coef[:, 1, n], att[:, n, 1 - n], ca1[:, 1 - n], ALU.mult)
                v.tensor_tensor(w2[:, n], att[:, n, n], sa[:, n], ALU.mult)
                ins = v.tensor_tensor(w3[:, n], att[:, n, 1 - n], sa[:, 1 - n], ALU.mult)
            link(ins)
            v.tensor_tensor(coef[:, 2], w2, w3, ALU.add).then_inc(coef_ready, 1)
            dve.wait_ge(coef_ready, 1)

            for k in range(KD):
                dve.wait_ge(u0_ready, k + 1)
                for n in range(NB):
                    ins = v.scalar_tensor_tensor(xbuf[1][:, 1, k, n, :], dbuf[:, 0, k, 1 - n, :], coef[:, 1, n, k:k + 1],
                                                 xbuf[1][:, 1, k, n, :], ALU.mult, ALU.add)
                link(ins)
                v.tensor_tensor(acc[:, k], xbuf[1][:, 1, k], xbuf[1][:, 0, k], ALU.add).then_inc(x20_ready, 1)
            dve.wait_ge(x20_ready, KD)
            v.nop().then_inc(next_free, 1)
            dve.wait_ge(mean20_mm, 1)
            v.scalar_tensor_tensor(tok(dbuf[:, 1]), bc(ps_mean2, KD), -1.0 / D, tok(acc), ALU.mult, ALU.add).then_inc(
                d20_ready, 1)
            dve.wait_ge(std_ready, 2 * NPAIR + 1)
            dve.wait_ge(stats_saved, 32 * NPAIR)
            link(v.reciprocal(rstd2, std2))
            for k in range(KD):
                link(v.tensor_tensor(tok(dbuf[:, 1])[:, k, :], tok(dbuf[:, 1])[:, k, :], rstd2, ALU.mult))
                for n in range(NB):
                    ins = v.tensor_scalar(dbuf[:, 1, k, n, :], dbuf[:, 1, k, n, :], cb1[:, n, k:k + 1],
                                          mod[:, 3, n, k:k + 1], ALU.mult, ALU.add)
                ins.then_inc(h20_ready, 1)
            for k in range(KD):
                dve.wait_ge(xn_hi_ready, k + 1)
                ins = v.tensor_tensor(xn_lo[:, k, :], tok(dbuf[:, 1])[:, k, :], xn_hi[:, k, :].bitcast(F32), ALU.subtract)
            ins.then_inc(xn_ready, 1)

            dve.sem_inc(gu_bank_free, 2)
            dve.sem_inc(y_bank_free, 2)
            dve.sem_inc(h_ready, 1)
            dve.sem_inc(acc_ready, KD)

            def split_lo(p, ahead, e):
                _, _, size = kind_of(p % NSLOT)
                r = p % 2
                dve.wait_ge(hi_ready, e * NSLOT + ahead + (p + 1))
                v.tensor_tensor(w_lo[r][:, 0:size], w_raw[r][:, 0:size], w_hi[r][:, 0:size].bitcast(F32),
                                ALU.subtract).then_inc(lo_ready, 1)

            split_lo(0, 0, 0)
            split_lo(1, 0, 0)

            def chunk(e, last):
                def one(p, ahead):
                    kind, n, _ = kind_of(p)
                    if kind == "gu":
                        i = n if n < HALF0 else n - HALF0
                        tile = bass.ds(ahead + i, 1)
                        dve.wait_ge(silu_done, e * NGU + ahead + (n + 1))
                        dve.wait_ge(h_ready, e * NGU + ahead + (n + 1))
                        v.tensor_tensor(prod[:], ps_up[n % 2], sg[n % 2][:], ALU.mult).then_inc(gu_bank_free, 1)
                        dve.wait_ge(gu_bank_free, e * NGU + ahead + (n + 3))
                        v.tensor_scalar(h_hi[:, tile, :].rearrange("p o t -> p (o t)"), prod[:], 1.0, None,
                                        ALU.mult).then_inc(h_hi_done, 1)
                        dve.wait_ge(h_hi_done, e * NGU + ahead + (n + 1))
                        v.tensor_tensor(h_lo[:, tile, :].rearrange("p o t -> p (o t)"), prod[:],
                                        h_hi[:, tile, :].rearrange("p o t -> p (o t)").bitcast(F32),
                                        ALU.subtract).then_inc(h_ready, 1)
                    elif kind == "tail":
                        dve.wait_ge(silu_done, e * NGU + (n + 1))
                        dve.wait_ge(h_ready, e * NGU + (n + 1))
                        v.tensor_tensor(prod[0:TAIL, :], ps_gate[n % 2][TAIL:P, :], sg[n % 2][0:TAIL, :],
                                        ALU.mult).then_inc(gu_bank_free, 1)
                        dve.wait_ge(gu_bank_free, e * NGU + (n + 3))
                        v.tensor_scalar(h_hi[0:TAIL, HT - 1, :], prod[0:TAIL, :], 1.0, None, ALU.mult).then_inc(h_hi_done, 1)
                        dve.wait_ge(h_hi_done, e * NGU + (n + 1))
                        v.tensor_tensor(h_hi[TAIL:P, HT - 1, :], prod[0:TAIL, :], h_hi[0:TAIL, HT - 1, :].bitcast(F32),
                                        ALU.subtract).then_inc(h_ready, 1)
                    else:
                        m = n % KD
                        if n < KD:
                            dve.wait_ge(acc_ready, e * KD + KD)
                        dve.wait_ge(slot_done, e * NSLOT + ahead + (p + 1))
                        for b in range(NB):
                            tile = acc[:, bass.ds(ahead + m, 1), b, :].rearrange("p o c -> p (o c)")
                            ins = v.scalar_tensor_tensor(tile, ps_y[n % 2][:, b * CC:(b + 1) * CC],
                                                         gate_a[:, 1, b, bass.ds(ahead + m, 1)], tile, ALU.mult, ALU.add)
                        ins.then_inc(y_bank_free, 1)
                    if not (last and p + 2 >= NSLOT):
                        split_lo(p + 2, ahead, e)
                    if p == P_TAIL - 2 and not last:
                        dve.wait_ge(std2_ready, e + 1)
                        v.reciprocal(rstd2, std2).then_inc(rstd2_ready, 1)
                    if p == P_DN1 and not last:
                        for k in range(KD):
                            dve.wait_ge(xn_hi_ready, e * KD + (KD + k + 1))
                            ins = v.tensor_tensor(xn_lo[:, k, :], tok(h_next)[:, k, :], xn_hi[:, k, :].bitcast(F32),
                                                  ALU.subtract)
                        ins.then_inc(xn_ready, 1)
                steps(dve, one)

            with dve.Fori(0, NCH - 1) as e:
                chunk(e, False)
            chunk(NCH - 1, True)

        @block.tensor
        def _(pe):
            mm = nc.tensor.matmul
            pe.wait_ge(ones_ready, 1)
            pe.wait_ge(silu_ready, 1)
            per_pair = NPART // NPAIR
            with pe.Fori(0, NPAIR // 2) as t:
                for u in range(2):
                    for h in range(2):
                        pe.wait_ge(presum_ready, t * 4 + (2 * u + h + 1))
                        pe.wait_ge(centred, t * 4 + 2 * u)
                        pe.wait_ge(mean_row_ready, t * 4 + 2 * u)
                        mm(ps_mean[h], ones[:], presum[:, h, :], start=True, stop=True).then_inc(mean_mm, 1)
                    for h in range(2):
                        pe.wait_ge(std_ready, t * 4 + 2 * u)
                        for k in range(KD):
                            n = (2 * u + h) * KD + k
                            pe.wait_ge(sq_ready, t * (4 * KD) + (n + 1))
                            mm(ps_var[h], ones[:], sq[:, n % SQ_RING, :], start=k == 0, stop=k == KD - 1).then_inc(sq_used, 1)
                    for j in range(per_pair):
                        w = per_pair * u + j
                        r = w % 2
                        pe.wait_ge(wm_loaded[r], t * (16 * per_pair) + (16 * (w // 2) + 16))
                        for l in range(LPP):
                            for k in range(KD):
                                col = t * (2 * per_pair * LPP * NB) + (w * LPP + l) * NB
                                ins = mm(ps_mod[:, bass.ds(col, NB)], wm[r][:, k, l * P:(l + 1) * P], silu_c[:, k, :],
                                         start=k == 0, stop=k == KD - 1)
                        ins.then_inc(mod_done, 1)

            for k in range(KD):
                pe.wait_ge(x20_ready, k + 1)
                ins = mm(ps_mean2, ones[:], tok(acc)[:, k, :], start=k == 0, stop=k == KD - 1)
            ins.then_inc(mean20_mm, 1)
            for k in range(KD):
                pe.wait_ge(sq_ready, NCH * KD + k + 1)
                mm(ps_var2, ones[:], sq[:, k % SQ_RING, :], start=k == 0, stop=k == KD - 1).then_inc(sq_used, 1)

            def gate_up(p, ahead, e):
                kind, n, _ = kind_of(p)
                r = p % 2
                if p < P_DN0:
                    pe.wait_ge(xn_ready, e + 1)
                pe.wait_ge(lo_ready, e * NSLOT + ahead + (p + 1))
                pe.wait_ge(gu_bank_free, e * NGU + ahead + (n + 1))
                for j, bank in enumerate((ps_gate[n % 2], ps_up[n % 2]) if kind == "gu" else (ps_gate[n % 2],)):
                    for k in range(KD):
                        w = slice((j * KD + k) * P, (j * KD + k + 1) * P)
                        mm(bank, w_hi[r][:, w], xn_hi[:, k, :], start=k == 0, stop=False)
                        mm(bank, w_hi[r][:, w], xn_lo[:, k, :], start=False, stop=False)
                        ins = mm(bank, w_lo[r][:, w], xn_hi[:, k, :], start=False, stop=k == KD - 1)
                ins.then_inc(slot_done, 1)

            def down(p, ahead, e):
                _, n, _ = kind_of(p)
                half = n // KD
                r = p % 2
                bank = ps_y[n % 2]
                pe.wait_ge(lo_ready, e * NSLOT + ahead + (p + 1))
                pe.wait_ge(y_bank_free, e * NDN + ahead + (n + 1))
                known = HALF0 if half == 0 else NGU
                pe.wait_ge(h_ready, e * NGU + known)
                for k in range(HT):
                    w = slice(k * P, (k + 1) * P)
                    if k == HT - 1:
                        pe.wait_ge(h_ready, e * NGU + (known + 1))
                    if half == 1 and k == HT - 1:
                        mm(bank, w_hi[r][:, w], h_hi[:, k, :], start=False, stop=False)
                        ins = mm(bank, w_lo[r][:, w], h_hi[:, k, :], start=False, stop=True)
                    else:
                        mm(bank, w_hi[r][:, w], h_hi[:, k, :], start=k == 0, stop=False)
                        mm(bank, w_hi[r][:, w], h_lo[:, k, :], start=False, stop=False)
                        ins = mm(bank, w_lo[r][:, w], h_hi[:, k, :], start=False, stop=k == HT - 1)
                ins.then_inc(slot_done, 1)

            def loop(slot, first, n, e):
                with pe.Fori(0, n // 2) as i:
                    for u in range(2):
                        slot(first + u, 2 * i, e)
                if n % 2:
                    slot(first + n - 1, 0, e)

            def chunk(e, last):
                loop(gate_up, 0, HALF0, e)
                loop(down, P_DN0, KD, e)
                if not last:
                    pe.wait_ge(sum2_ready, e + 1)
                    mm(ps_mean2, ones[:], pool_acc, start=True, stop=True).then_inc(stat2_mm, 1)
                loop(gate_up, P_GU1, HALF1 - 1, e)
                if not last:
                    pe.wait_ge(sq2_ready, e + 1)
                    mm(ps_var2, ones[:], pool_acc, start=True, stop=True).then_inc(stat2_mm, 1)
                gate_up(P_TAIL - 1, 0, e)
                gate_up(P_TAIL, 0, e)
                loop(down, P_DN1, KD, e)

            with pe.Fori(0, NCH - 1) as e:
                chunk(e, False)
            chunk(NCH - 1, True)


def chunks_of(a):
    return np.ascontiguousarray(a.reshape(NB, NCH, CC, KD, P).transpose(1, 4, 3, 0, 2)).reshape(NCH, P, KD * T)


def tiles_of(w, n):
    return w.reshape(n, KD, P).transpose(2, 1, 0)


def kernel(L0_attn_x, L0_ffn_W_gate, L0_ffn_W_up, L0_ffn_W_down, L0_c, L0_wmod):
    import concourse.bacc as bacc
    from concourse.bass_utils import run_bass_kernel_spmd

    xin, wg, wu, wd, c, wmod = (np.asarray(a) for a in (L0_attn_x, L0_ffn_W_gate, L0_ffn_W_up, L0_ffn_W_down, L0_c, L0_wmod))
    whole = FT * P
    gu = np.stack([np.stack([tiles_of(w[f * P:(f + 1) * P], P) for w in (wg, wu)], 1) for f in range(FT)])
    gut = np.concatenate([tiles_of(wg[whole:], TAIL), tiles_of(wu[whole:], TAIL)], 2)
    wdt = wd.T
    blocks = [wdt[f * P:(f + 1) * P] for f in range(FT)] + [np.concatenate([wdt[whole:], wdt[whole:]], 0)]
    halves = [np.stack(blocks[:HALF0]), np.stack(blocks[HALF0:])]
    dn = np.stack([h.reshape(HT, P, KD, P).transpose(2, 1, 0, 3) for h in halves])
    arrays = {
        "x": chunks_of(xin),
        "wgu": np.ascontiguousarray(gu).reshape(FT, P, GU),
        "wgut": np.ascontiguousarray(gut).reshape(1, P, GUT),
        "wdn": np.ascontiguousarray(dn).reshape(NDN, P, DN),
        "cT": np.ascontiguousarray(c.reshape(NB, KD, P).transpose(2, 1, 0)),
        "wmod": np.ascontiguousarray(wmod.reshape(KD, P, NPART, WPART).transpose(2, 1, 0, 3)),
    }
    nc = bacc.Bacc("TRN2", target_bir_lowering=False, num_devices=1)
    args = [nc.dram_tensor(n, a.shape, mybir.dt.from_np(a.dtype), kind="ExternalInput").ap() for n, a in arrays.items()]
    out = nc.dram_tensor("out", (NCH, P, KD * T), F32, kind="ExternalOutput").ap()
    build(nc, *args, out)
    r = run_bass_kernel_spmd(nc, [arrays], core_ids=[0])
    y = r.results[0]["out"].reshape(NCH, P, KD, NB, CC)
    return np.ascontiguousarray(y.transpose(3, 0, 4, 2, 1)).reshape(NB, C, D)
```

```python
import numpy as np

import concourse.bass as bass
from concourse import mybir
from concourse.alu_op_type import AluOpType as ALU

F32 = mybir.dt.float32
F32R = mybir.dt.float32r
ACT = mybir.ActivationFunctionType

P = 128
NB = 2
D = 1024
C = 2048
F = 2752
KD = D // P
CC = 256
T = NB * CC
NCH = C // CC
NPAIR = NCH // 2
NMOD = 6
FT = F // P
TAIL = F - FT * P
assert 2 * TAIL == P
HALF0 = (FT + 1) // 2
HALF1 = FT - HALF0
HT = HALF0
assert HALF1 + 1 == HT
GU = 2 * KD * P
GUT = KD * P
DN = HT * P
NGU = FT + 1
NDN = 2 * KD
NSLOT = NGU + NDN
P_DN0 = HALF0
P_GU1 = P_DN0 + KD
P_TAIL = P_GU1 + HALF1
P_DN1 = P_TAIL + 1
assert NSLOT == P_DN1 + KD and NSLOT % 2 == 0 and NGU % 2 == 0
WPART = 256
NPART = NMOD * D // WPART
WM_RING = 3
BLOCK = 512
NCOL = BLOCK // P
GROUP = [6, 6, 8, 4]
FIRST = [sum(GROUP[:i]) for i in range(len(GROUP))]
ROWS = [n * WPART // BLOCK * NB for n in GROUP]
SQ_PER = 2
NSQ = KD // SQ_PER
PRE = 6
SQ_PRE = 3
assert NPAIR == 4 and sum(GROUP) == NPART and 2 * WPART == BLOCK and GROUP[0] == GROUP[1] == 2 * WM_RING
EPS = 1e-5
GATE_MIN = 0.25
SCORE_SCALE = float(np.float32(1.0) / np.sqrt(np.float32(C)))


def build(nc, x, wgu, wgut, wdn, cT, eye, wmod, out):
    base = (nc.sbuf_base + 63) // 64 * 64
    K = 1024

    def sb(name, shape, dt, at):
        return nc.alloc_sbuf_tensor_at(name, [P] + shape, dt, offset=base + at)

    xbuf = [sb("xbuf0", [2, KD, NB, CC], F32, 32 * K), sb("xbuf1", [2, KD, NB, CC], F32, 64 * K)]
    dbuf = [sb("dbuf0", [2, KD, NB, CC], F32, 96 * K), sb("dbuf1", [2, KD, NB, CC], F32, 0)]
    x2_next = sb("x2_next", [KD, NB, CC], F32, 0)
    h_next = sb("h_next", [KD, NB, CC], F32, 16 * K)
    h_hi = sb("h_hi", [HT, T], F32R, 32 * K)
    h_lo = sb("h_lo", [HT, T], F32R, 54 * K)
    xn_hi = sb("xn_hi", [KD, T], F32R, 76 * K)
    xn_lo = sb("xn_lo", [KD, T], F32R, 92 * K)
    acc = sb("acc", [KD, NB, CC], F32, 108 * K)
    w_hi = [sb(f"w_hi{r}", [GU], F32R, (124 + 24 * r) * K) for r in range(2)]
    w_lo = [sb(f"w_lo{r}", [GU], F32R, (132 + 24 * r) * K) for r in range(2)]
    w_raw = [sb(f"w_raw{r}", [GU], F32, (140 + 24 * r) * K) for r in range(2)]
    mean = sb("mean", [2, 2, T], F32, 128 * K)
    sq_pair = sb("sq_pair", [2, T], F32, 136 * K)
    wm = [sb(f"wm{r}", [KD, WPART], F32, (148 + 8 * r) * K) for r in range(WM_RING)]
    sq = sb("sq", [2, SQ_PER, T], F32, 172 * K)
    sg = [sb(f"sg{r}", [T], F32, (172 + 2 * r) * K) for r in range(2)]
    prod = sb("prod", [T], F32, 176 * K)
    at = [180 * K]

    def small(name, shape, dt=F32):
        size = int(np.prod(shape)) * 4
        t = sb(name, shape, dt, at[0])
        at[0] += (size + 31) // 32 * 32
        return t

    presum = small("presum", [2, T])
    rstd = small("rstd", [2, 2, T])
    std = small("std", [2, T])
    junk_a = small("junk_a", [2, 2, CC])
    junk_v = small("junk_v", [2, 2, CC])
    ones = small("ones", [P])
    eye_t = small("eye_t", [max(ROWS)])
    ct = small("ct", [KD, NB])
    silu_pad = small("silu_pad", [KD, 2 * max(ROWS) - NB])
    eps_t = small("eps_t", [1])
    part = small("part", [2, 5, KD])
    sums = small("sums", [2, 5, KD])
    xs = small("xs", [5, KD])
    mod = small("mod", [NMOD, NB, KD])
    ca1 = small("ca1", [NB, KD])
    cb1 = small("cb1", [NB, KD])
    gate_a = small("gate_a", [2, NB, KD])
    gate_t = small("gate_t", [2, NB, KD])
    score = small("score", [NB, NB, KD])
    prob = small("prob", [NB, NB, KD])
    tmp = [small(f"tmp{i}", [NB, KD]) for i in range(5)]
    att = small("att", [NB, NB, KD])
    coef = small("coef", [3, NB, KD])
    mod_rows = [presum[:, i, :] for i in range(2)]
    pool_u, pool_v = presum[:, 0, :], presum[:, 1, :]
    pool_acc, pool_sq = std[:, 0, :], std[:, 1, :]
    stat1 = junk_a[:].rearrange("p r h c -> p r (h c)")
    mean2, std2, rstd2 = rstd[:, 0, 0, :], rstd[:, 0, 1, :], rstd[:, 1, 0, :]
    x_0, xhat_0, u_0, d_0 = xbuf[1][:, 0], dbuf[1][:, 0], xbuf[0][:, 0], xbuf[0][:, 1]

    assert base + at[0] <= nc.sbuf_usable_end, (base + at[0], nc.sbuf_usable_end)
    ps = nc.alloc_psum_tensor("ps", [P, 8, T], F32)
    ps_mean, ps_var = [ps[:, 0, :], ps[:, 1, :]], [ps[:, 6, :], ps[:, 7, :]]
    ps_rows, ps_mod = [ps[:, 4, :], ps[:, 5, :], ps[:, 3, :], ps[:, 5, :]], [ps[:, 2, :], ps[:, 4, :], ps[:, 2, :]]
    ps_gate, ps_up, ps_y = [ps[:, 0, :], ps[:, 1, :]], [ps[:, 2, :], ps[:, 3, :]], [ps[:, 4, :], ps[:, 5, :]]
    ps_mean2, ps_var2 = ps[:, 6, :], ps[:, 7, :]

    stats_dram = nc.dram_tensor("stats", [NCH, 2, T], F32, kind="Internal").ap()

    sem = nc.alloc_semaphore
    c_loaded, eye_loaded, eps_ready, ones_ready = sem("c_loaded"), sem("eye_loaded"), sem("eps_ready"), sem("ones_ready")
    x_loaded = [[sem(f"x_loaded{u}{h}") for h in range(2)] for u in range(2)]
    presum_ready, mean_mm, mean_ready = sem("presum_ready"), sem("mean_mm"), sem("mean_ready")
    centred, sq_ready, sq_added = sem("centred"), sem("sq_ready"), sem("sq_added")
    sq_pair_used, sum_done = sem("sq_pair_used"), sem("sum_done")
    std_ready, rstd_ready = sem("std_ready"), sem("rstd_ready")
    mean_saved, rstd_saved = ([sem(f"{w}_saved{u}") for u in range(2)] for w in ("mean", "rstd"))
    xhat_ready, sqsum_done, cross_done = sem("xhat_ready"), sem("sqsum_done"), sem("cross_done")
    wm_loaded = [sem(f"wm_loaded{r}") for r in range(WM_RING)]
    silu_zeroed, silu_ready, mod_done = sem("silu_zeroed"), sem("silu_ready"), sem("mod_done")
    rows_copied, mod_ready = sem("rows_copied"), sem("mod_ready")
    sums_ready = sem("sums_ready")
    shifted, exp_done, coef_ready = sem("shifted"), sem("exp_done"), sem("coef_ready")
    u0_ready, x20_ready, d20_ready, t20_ready = sem("u0_ready"), sem("x20_ready"), sem("d20_ready"), sem("t20_ready")
    dve_chain, pool_chain, pool_passed = sem("dve_chain"), sem("pool_chain"), sem("pool_passed")
    pe_passed = sem("pe_passed")
    raw_loaded = [sem(f"raw_loaded{r}") for r in range(2)]
    hi_ready, lo_ready, slot_done = sem("hi_ready"), sem("lo_ready"), sem("slot_done")
    gu_bank_free, y_bank_free = sem("gu_bank_free"), sem("y_bank_free")
    silu_done, h_hi_done, h_ready = sem("silu_done"), sem("h_hi_done"), sem("h_ready")
    xn_hi_ready, xn_ready = sem("xn_hi_ready"), sem("xn_ready")
    next_free, next_x, next_stat = sem("next_free"), sem("next_x"), sem("next_stat")
    acc_ready, out_stored = sem("acc_ready"), sem("out_stored")
    sum2_ready, sq2_ready, stat2_mm = sem("sum2_ready"), sem("sq2_ready"), sem("stat2_mm")
    sq20_ready, sq20_used, mean20_mm, std20_ready = sem("sq20_ready"), sem("sq20_used"), sem("mean20_mm"), sem("std20_ready")
    mean2_ready, std2_ready, rstd2_ready, h_next_ready = (
        sem("mean2_ready"), sem("std2_ready"), sem("rstd2_ready"), sem("h_next_ready"))

    def bc(ap, n):
        return ap[:, None, :].broadcast_to([P, n, T])

    def tok(ap):
        return ap.rearrange("p k b c -> p k (b c)")

    def kind_of(p):
        if p < P_DN0:
            return "gu", p, GU
        if p < P_GU1:
            return "dn", p - P_DN0, DN
        if p < P_TAIL:
            return "gu", p - KD, GU
        if p == P_TAIL:
            return "tail", FT, GUT
        return "dn", p - P_DN1 + KD, DN

    STEPS = []
    for first, end in ((0, 2), (2, P_DN0), (P_DN0, P_GU1), (P_GU1, P_TAIL), (P_TAIL, P_DN1), (P_DN1, P_DN1 + 1), (P_DN1 + 1, NSLOT)):
        n = max(0, (end - first - 2) // 2)
        if n:
            STEPS.append((first, n, 2))
        STEPS += [(p, 1, 1) for p in range(first + 2 * n, end)]

    def steps(eng, one):
        for first, n, per in STEPS:
            if n > 1:
                with eng.Fori(0, n) as i:
                    for u in range(per):
                        one(first + u, 2 * i)
            else:
                one(first, 0)

    block = nc.Block()
    with block as block:

        @block.sync
        def _(sp):
            def load_part(w):
                if w >= WM_RING:
                    sp.wait_ge(mod_done, w - WM_RING + 1)
                sp.dma_start(wm[w % WM_RING][:], wmod[w]).then_inc(wm_loaded[w % WM_RING], 16)

            def load_pair(a):
                if a >= 2:
                    sp.wait_ge(centred, 4 * (a - 1))
                chunk = 2 * ((a + 1) % NPAIR)
                for h in range(2):
                    sp.dma_start(tok(xbuf[a % 2][:, h]), x[chunk + h].rearrange("p (k t) -> p k t", k=KD)).then_inc(
                        x_loaded[a % 2][h], 16)

            load_pair(0)
            sp.dma_start(ct[:], cT).then_inc(c_loaded, 16)
            sp.dma_start(eye_t[0:max(ROWS), :], eye).then_inc(eye_loaded, 16)
            for a in range(1, NPAIR):
                load_pair(a)
                for w in range(WM_RING * (a - 1), WM_RING * a):
                    load_part(w)
            def load_slot(p, ahead, e):
                kind, n, size = kind_of(p % NSLOT)
                r = p % 2
                if not (isinstance(e, int) and e == 0 and isinstance(ahead, int) and p < 2):
                    sp.wait_ge(lo_ready, e * NSLOT + ahead + (p - 1))
                if kind == "gu":
                    src = wgu[bass.ds(ahead + n, 1), :, :]
                elif kind == "tail":
                    src = wgut[0:1, :, :]
                else:
                    src = wdn[bass.ds(ahead + n, 1), :, :]
                sp.dma_start(w_raw[r][:, 0:size], src.rearrange("o p w -> (o p) w")).then_inc(raw_loaded[r], 16)

            for w in range(WM_RING * (NPAIR - 1), FIRST[3]):
                load_part(w)
            load_slot(0, 0, 0)
            for w in range(FIRST[3], NPART):
                load_part(w)
            sp.wait_ge(mod_done, NPART)
            load_slot(1, 0, 0)
            for u in range(2):
                sp.wait_ge(mean_saved[u], 16 + 16 * (NPAIR // 2))
                sp.wait_ge(rstd_saved[u], 16 + 16 * (NPAIR // 2))

            def store(p, ahead, e):
                m = p - P_DN1
                sp.wait_ge(y_bank_free, e * NDN + ahead + (2 + KD + m + 1))
                sp.dma_start(out[bass.ds(e, 1), :, bass.ds((ahead + m) * T, T)].rearrange("o p t -> (o p) t"),
                             acc[:, bass.ds(ahead + m, 1), :, :].rearrange("p o b c -> p (o b c)")).then_inc(out_stored, 16)

            def chunk(e, last):
                def one(p, ahead):
                    if not (last and p + 2 >= NSLOT):
                        load_slot(p + 2, ahead, e)
                    if p > P_DN1:
                        store(p - 1, ahead, e)
                    if p == 1 and not last:
                        sp.wait_ge(next_free, e + 1)
                        sp.dma_start(x2_next[:].rearrange("p k b c -> p (k b c)"),
                                     x[bass.ds(e + 1, 1), :, :].rearrange("o p w -> (o p) w")).then_inc(next_x, 16)
                        sp.dma_start(stat1.rearrange("p s t -> p (s t)"),
                                     stats_dram[bass.ds(e + 1, 1), :, :].rearrange("o s t -> o (s t)").broadcast_to(
                                         [P, 2 * T])).then_inc(next_stat, 16)
                steps(sp, one)
                store(NSLOT - 1, 0, e)

            with sp.Fori(0, NCH - 1) as e:
                chunk(e, False)
            chunk(NCH - 1, True)
            sp.wait_ge(out_stored, 16 * KD * NCH)

        @block.gpsimd
        def _(pool):
            g = nc.gpsimd
            g.memset(ones[:], 1.0).then_inc(ones_ready, 1)
            g.memset(silu_pad[:], 0.0).then_inc(silu_zeroed, 1)
            pool.sem_inc(sq_added, 1)

            links_of = PRE - 2
            with pool.Fori(0, NPAIR // 2) as t:
                def presums(u, h):
                    i = 2 * u + h
                    pool.wait_ge(x_loaded[u][h], t * 16 + 16)
                    pool.wait_ge(mean_mm, t * 4 + (i + 1))
                    xk = tok(xbuf[u][:, h])
                    for k in range(1, PRE):
                        ins = g.tensor_tensor(presum[:, h, :], xk[:, 0, :] if k == 1 else presum[:, h, :], xk[:, k, :], ALU.add)
                        if k < PRE - 1:
                            ins.then_inc(pool_chain, 1)
                            pool.wait_ge(pool_chain, t * (4 * links_of) + (i * links_of + k))
                        else:
                            ins.then_inc(presum_ready, 1)

                def add_squares(u, h):
                    i = 2 * u + h
                    for j in range(SQ_PRE):
                        m = i * SQ_PRE + j
                        pool.wait_ge(sq_ready, t * (4 * NSQ) + (i * NSQ + j + 1))
                        pool.wait_ge(sq_pair_used, t * (4 * SQ_PRE) + (m + 1))
                        g.tensor_tensor(sq_pair[:, m % 2, :], sq[:, j % 2, 0, :], sq[:, j % 2, 1, :], ALU.add).then_inc(
                            sq_added, 1)

                presums(0, 0)
                presums(0, 1)
                presums(1, 0)
                add_squares(0, 0)
                presums(1, 1)
                add_squares(0, 1)
                add_squares(1, 0)
                add_squares(1, 1)

            chain0 = NCH * links_of

            def chunk(e, first):
                count = [0]
                total = chunk_links

                def pause(sem_, value):
                    pool.wait_ge(sem_, value)
                    pool.sem_inc(pool_passed, 1)

                def link(ins):
                    ins.then_inc(pool_chain, 1)
                    count[0] += 1
                    pause(pool_chain, e * total + (chain0 + count[0]))

                if not first:
                    pause(out_stored, e * (16 * KD))
                    for k in range(KD):
                        ins = g.tensor_copy(tok(acc)[:, k, :], tok(x2_next)[:, k, :])
                        if k < KD - 1:
                            ins.then_inc(acc_ready, 1)
                    link(ins)
                    pool.nop().then_inc(acc_ready, 1)
                    pool.nop().then_inc(next_free, 1)
                pool.wait_ge(next_x, e * 16 + 16)
                pool.wait_ge(next_stat, e * 16 + 16)
                pool.wait_ge(xn_ready, e * KD + KD)
                hk, xk = tok(h_next), tok(x2_next)
                for k in range(KD):
                    link(g.tensor_tensor(hk[:, k, :], xk[:, k, :], stat1[:, 0, :], ALU.subtract))
                    link(g.tensor_tensor(hk[:, k, :], hk[:, k, :], stat1[:, 1, :], ALU.mult))
                    for n in range(NB):
                        cols = slice(n * CC, (n + 1) * CC)
                        g.tensor_scalar(pool_u[:, cols], h_next[:, k, n, :], coef[:, 0, n, k:k + 1],
                                        coef[:, 2, n, k:k + 1], ALU.mult, ALU.add)
                        ins = g.tensor_scalar(pool_v[:, cols], h_next[:, k, 1 - n, :], coef[:, 1, n, k:k + 1], 0.0,
                                              ALU.mult, ALU.add)
                    link(ins)
                    link(g.tensor_tensor(pool_u, pool_u, pool_v, ALU.add))
                    link(g.tensor_tensor(xk[:, k, :], xk[:, k, :], pool_u, ALU.add))
                    if k == 0:
                        if not first:
                            pause(stat2_mm, e * 2)
                        link(g.tensor_copy(pool_acc, xk[:, 0, :]))
                    elif k < KD - 1:
                        link(g.tensor_tensor(pool_acc, pool_acc, xk[:, k, :], ALU.add))
                    else:
                        g.tensor_tensor(pool_acc, pool_acc, xk[:, k, :], ALU.add).then_inc(sum2_ready, 1)
                pool.wait_ge(mean2_ready, e + 1)
                for k in range(KD):
                    link(g.tensor_tensor(hk[:, k, :], xk[:, k, :], mean2, ALU.subtract))
                    if k == 0:
                        link(g.tensor_tensor(pool_acc, hk[:, 0, :], hk[:, 0, :], ALU.mult))
                    else:
                        link(g.tensor_tensor(pool_sq, hk[:, k, :], hk[:, k, :], ALU.mult))
                        ins = g.tensor_tensor(pool_acc, pool_acc, pool_sq, ALU.add)
                        if k < KD - 1:
                            link(ins)
                        else:
                            ins.then_inc(sq2_ready, 1)
                pool.wait_ge(rstd2_ready, e + 1)
                for k in range(KD):
                    link(g.tensor_tensor(hk[:, k, :], hk[:, k, :], rstd2, ALU.mult))
                    for n in range(NB):
                        ins = g.tensor_scalar(h_next[:, k, n, :], h_next[:, k, n, :], cb1[:, n, k:k + 1],
                                              mod[:, 3, n, k:k + 1], ALU.mult, ALU.add)
                    link(ins)
                pool.nop().then_inc(h_next_ready, 1)
                return count[0]

            chunk_links = (6 * KD - 1) + (3 * KD - 2) + 2 * KD + 1
            pool.wait_ge(coef_ready, 1)
            assert chunk(0, True) == chunk_links - 1
            chain0 -= 1
            with pool.Fori(1, NCH - 1) as e:
                n = chunk(e, False)
            assert n == chunk_links
            pool.wait_ge(out_stored, (NCH - 1) * 16 * KD)
            for k in range(KD):
                g.tensor_copy(tok(acc)[:, k, :], tok(x2_next)[:, k, :]).then_inc(acc_ready, 1)

        @block.scalar
        def _(act):
            s = nc.scalar
            act.wait_ge(c_loaded, 16)
            act.wait_ge(silu_zeroed, 1)
            s.activation(silu_pad[:, :, max(ROWS) - NB:max(ROWS)], ct[:], ACT.Silu).then_inc(silu_ready, 1)
            act.wait_ge(eps_ready, 1)

            for u in range(2):
                act.sem_inc(mean_saved[u], 16)
                act.sem_inc(rstd_saved[u], 16)
            act.sem_inc(mean_ready, 2)
            act.sem_inc(std_ready, 2)
            act.sem_inc(sqsum_done, 4 * KD)

            with act.Fori(0, NPAIR // 2) as t:
                def copy_mean(u, h):
                    act.wait_ge(mean_mm, t * 4 + (2 * u + h + 3))
                    act.wait_ge(mean_saved[u], t * 16 + 16)
                    s.mul(mean[:, u, h, :], ps_mean[h], 1.0 / D).then_inc(mean_ready, 1)

                def save(u, which, rows, ready, saved):
                    act.wait_ge(ready, t * 4 + (2 * u + 4))
                    chunk = t * 4 + 2 if u == 0 else t * -4 + 4
                    s.dma_start(stats_dram[bass.ds(chunk, 2), which, :].rearrange("(o h) t -> o h t", o=1),
                                rows[0:1, u]).then_inc(saved[u], 16)

                def square(u, h, js):
                    i = 2 * u + h
                    for j in js:
                        act.wait_ge(centred, t * 8 + (2 * i + j * 2 // NSQ + 1))
                        if j == 1:
                            act.wait_ge(sum_done, t * 4 + (i + 1))
                        else:
                            act.wait_ge(sq_added, t * (4 * SQ_PRE) + (i * SQ_PRE + max(0, j - 1) + 1))
                        s.activation(sq[:, j % 2], tok(dbuf[u][:, h])[:, j * SQ_PER:(j + 1) * SQ_PER, :], ACT.Square).then_inc(
                            sq_ready, 1)

                def root(u, h):
                    i = 2 * u + h
                    act.wait_ge(sum_done, t * 4 + (i + 2))
                    act.wait_ge(rstd_ready, t * 4 + (i + 1))
                    s.activation(std[:, h, :], ps_var[h], ACT.Sqrt, bias=eps_t[:, 0:1], scale=1.0 / D).then_inc(std_ready, 1)

                def square_sums(u, ks):
                    for k in ks:
                        for b in range(NB):
                            n = 2 * u * KD + NB * k + b
                            act.wait_ge(xhat_ready, t * (4 * KD) + (n + 1))
                            act.wait_ge(sqsum_done, t * (4 * KD) + (4 * KD + n - 1))
                            s.activation(junk_a[:, b], dbuf[u][:, :, k, b, :], ACT.Square,
                                         accum_out=part[:, u, 2 + b, k:k + 1]).then_inc(sqsum_done, 1)

                first, second = range(NSQ // 2), range(NSQ // 2, NSQ)
                copy_mean(0, 0)
                square(0, 0, first)
                copy_mean(0, 1)
                save(0, 0, mean, mean_ready, mean_saved)
                square(0, 0, second)
                square(0, 1, first)
                copy_mean(1, 0)
                root(0, 0)
                square(0, 1, second)
                square(1, 0, first)
                copy_mean(1, 1)
                save(1, 0, mean, mean_ready, mean_saved)
                root(0, 1)
                square(1, 0, second)
                square(1, 1, first)
                root(1, 0)
                square(1, 1, second)
                root(1, 1)
                save(0, 1, rstd, rstd_ready, rstd_saved)
                square_sums(0, range(KD))
                save(1, 1, rstd, rstd_ready, rstd_saved)
                square_sums(1, range(KD))

            def copy_rows(i):
                act.wait_ge(mod_done, FIRST[i] + GROUP[i])
                if i >= 2:
                    act.wait_ge(mod_ready, i - 1)
                s.copy(mod_rows[i % 2][0:ROWS[i], :], ps_rows[i][0:ROWS[i], :]).then_inc(rows_copied, 1)

            copy_rows(0)
            copy_rows(1)

            act.wait_ge(shifted, 1)
            s.activation(prob[:], score[:], ACT.Exp).then_inc(exp_done, 1)

            def split_hi(p, ahead, e):
                _, _, size = kind_of(p % NSLOT)
                r = p % 2
                act.wait_ge(raw_loaded[r], e * (8 * NSLOT) + 8 * ahead + (16 * (p // 2) + 16))
                if p >= 2:
                    act.wait_ge(slot_done, e * NSLOT + ahead + (p - 1))
                s.copy(w_hi[r][:, 0:size], w_raw[r][:, 0:size]).then_inc(hi_ready, 1)

            act.wait_ge(coef_ready, 1)
            for k in range(KD):
                for n in range(NB):
                    ins = s.activation(u_0[:, k, n, :], xhat_0[:, k, n, :], ACT.Identity,
                                       bias=coef[:, 2, n, k:k + 1], scale=coef[:, 0, n, k:k + 1])
                ins.then_inc(u0_ready, 1)
            for u in range(2):
                act.wait_ge(mean_saved[u], 16 + 16 * (NPAIR // 2))
                act.wait_ge(rstd_saved[u], 16 + 16 * (NPAIR // 2))
            split_hi(0, 0, 0)
            copy_rows(2)
            for j in range(NSQ):
                act.wait_ge(d20_ready, 1 + j * 2 // NSQ)
                if j >= 2:
                    act.wait_ge(sq20_used, j - 1)
                s.activation(sq[:, j % 2], tok(d_0)[:, j * SQ_PER:(j + 1) * SQ_PER, :], ACT.Square).then_inc(sq20_ready, 1)
            act.wait_ge(sq20_used, NSQ)
            s.activation(std2, ps_var2, ACT.Sqrt, bias=eps_t[:, 0:1], scale=1.0 / D).then_inc(std20_ready, 1)

            for k in range(KD):
                act.wait_ge(t20_ready, k + 1)
                for n in range(NB):
                    ins = s.activation(xn_hi[:, k, n * CC:(n + 1) * CC], d_0[:, k, n, :], ACT.Identity,
                                       bias=mod[:, 3, n, k:k + 1])
                ins.then_inc(xn_hi_ready, 1)
            copy_rows(3)
            split_hi(1, 0, 0)

            def chunk(e, last):
                def one(p, ahead):
                    kind, n, _ = kind_of(p)
                    if kind != "dn":
                        rows = P if kind == "gu" else TAIL
                        act.wait_ge(slot_done, e * NSLOT + ahead + (p + 1))
                        act.wait_ge(gu_bank_free, e * NGU + ahead + (n + 1))
                        s.activation(sg[n % 2][0:rows, :], ps_gate[n % 2][0:rows, :], ACT.Silu).then_inc(silu_done, 1)
                    if not (last and p + 2 >= NSLOT):
                        split_hi(p + 2, ahead, e)
                    if p == P_GU1 - 1 and not last:
                        act.wait_ge(stat2_mm, e * 2 + 1)
                        s.mul(mean2, ps_mean2, 1.0 / D).then_inc(mean2_ready, 1)
                    if p == P_TAIL - 2 and not last:
                        act.wait_ge(stat2_mm, e * 2 + 2)
                        s.activation(std2, ps_var2, ACT.Sqrt, bias=eps_t[:, 0:1], scale=1.0 / D).then_inc(std2_ready, 1)
                    if p == P_DN1 and not last:
                        act.wait_ge(h_next_ready, e + 1)
                        for k in range(KD):
                            s.copy(xn_hi[:, k, :], tok(h_next)[:, k, :]).then_inc(xn_hi_ready, 1)
                steps(act, one)

            with act.Fori(0, NCH - 1) as e:
                chunk(e, False)
            chunk(NCH - 1, True)

        @block.vector
        def _(dve):
            v = nc.vector
            v.memset(eps_t[:], EPS).then_inc(eps_ready, 1)
            v.memset(sums[:], 0.0).then_inc(sums_ready, 1)
            v.memset(part[:], 0.0).then_inc(sums_ready, 1)
            dve.sem_inc(rstd_ready, 2)
            dve.sem_inc(cross_done, 2 * KD)
            dve.wait_ge(sums_ready, 2)

            with dve.Fori(0, NPAIR // 2) as t:
                def centre(u, h):
                    i = 2 * u + h
                    dve.wait_ge(mean_ready, t * 4 + (i + 3))
                    dve.wait_ge(sqsum_done, t * (4 * KD) + 2 * KD * (u + 1))
                    dve.wait_ge(cross_done, t * (2 * KD) + KD * (u + 1))
                    for q in range(2):
                        ks = slice(q * KD // 2, (q + 1) * KD // 2)
                        v.tensor_tensor(tok(dbuf[u][:, h])[:, ks], tok(xbuf[u][:, h])[:, ks], bc(mean[:, u, h, :], KD // 2),
                                        ALU.subtract).then_inc(centred, 1)

                def invert(u, h):
                    dve.wait_ge(std_ready, t * 4 + (2 * u + h + 3))
                    dve.wait_ge(rstd_saved[u], t * 16 + 16)
                    v.reciprocal(rstd[:, u, h, :], std[:, h, :]).then_inc(rstd_ready, 1)

                def normalise(u, k):
                    for b in range(NB):
                        v.scalar_tensor_tensor(dbuf[u][:, :, k, b, :], dbuf[u][:, :, k, b, :], 1.0,
                                               rstd[:, u, :, b * CC:(b + 1) * CC], ALU.mult, ALU.mult,
                                               accum_out=part[:, u, b, k:k + 1]).then_inc(xhat_ready, 1)

                def cross(u, k):
                    n = KD * u + k
                    dve.wait_ge(xhat_ready, t * (4 * KD) + NB * (n + 1))
                    dve.wait_ge(cross_done, t * (2 * KD) + (2 * KD + n - 1))
                    v.tensor_tensor_reduce(junk_v[:, k % 2], dbuf[u][:, :, k, 0, :], dbuf[u][:, :, k, 1, :], 1.0, 0.0, ALU.mult,
                                           ALU.add, accum_out=part[:, u, 4, k:k + 1]).then_inc(cross_done, 1)

                centre(0, 0)
                centre(0, 1)
                centre(1, 0)
                invert(0, 0)
                centre(1, 1)
                invert(0, 1)
                dve.wait_ge(sums_ready, t + 2)
                v.tensor_tensor(sums[:], sums[:], part[:], ALU.add).then_inc(sums_ready, 1)
                dve.wait_ge(sums_ready, t + 3)
                for u in range(2):
                    dve.wait_ge(rstd_ready, t * 4 + (2 * u + 4))
                    for k in range(KD):
                        normalise(u, k)
                        if k:
                            cross(u, k - 1)
                        if u == 0 and k in (2, 4):
                            invert(1, (k - 2) // 2)
                    cross(u, KD - 1)

            links = [0]

            def link(ins):
                ins.then_inc(dve_chain, 1)
                links[0] += 1
                dve.wait_ge(dve_chain, links[0])

            half = NMOD // 2

            def take(turned, bank, rows, first, last):
                dve.wait_ge(mod_ready, turned)
                columns = bank[:, 0:NCOL * rows].rearrange("p (c i b n) -> p i n b c", c=NCOL, b=D // BLOCK, n=NB)
                for i in range(first, last):
                    ins = v.tensor_copy(mod[:, i].rearrange("p n (b c) -> p n b c", c=NCOL), columns[:, i - first])
                link(ins)

            def gate(j):
                link(v.tensor_scalar(gate_t[:, j], mod[:, half * j + 2], 0.0, 2.0, ALU.is_ge, ALU.mult))
                link(v.tensor_scalar(gate_t[:, j], gate_t[:, j], -1.0, None, ALU.add))
                link(v.tensor_tensor(gate_a[:, j], mod[:, half * j + 2], gate_t[:, j], ALU.mult))
                link(v.scalar_tensor_tensor(gate_a[:, j], gate_a[:, j], GATE_MIN, gate_t[:, j], ALU.max, ALU.mult))

            take(2, ps_mod[0], ROWS[0] + ROWS[1], 0, half)
            v.tensor_scalar(ca1[:], mod[:, 1], 1.0, None, ALU.add)
            gate(0)

            dve.wait_ge(sqsum_done, (NPAIR + 2) * 2 * KD)
            dve.wait_ge(cross_done, (NPAIR + 2) * KD)
            link(v.tensor_tensor(sums[:], sums[:], part[:], ALU.add))
            link(v.tensor_tensor(xs[:], sums[:, 0], sums[:, 1], ALU.add))
            sa = mod[:, 0]
            w0, w1, w2, w3, w4 = (t_[:] for t_ in tmp)
            v.tensor_tensor(w0, ca1[:], xs[:, 2:4], ALU.mult)
            v.tensor_tensor(w1, sa, xs[:, 0:2], ALU.mult)
            v.tensor_tensor(w2, sa, sa, ALU.mult)
            v.tensor_tensor(w3[:, 0], ca1[:, 1], xs[:, 4], ALU.mult)
            link(v.tensor_tensor(w3[:, 1], ca1[:, 1], xs[:, 1], ALU.mult))
            v.scalar_tensor_tensor(w0, w1, 2.0, w0, ALU.mult, ALU.add)
            v.tensor_tensor(w4[:, 0], sa[:, 1], xs[:, 0], ALU.mult)
            link(v.tensor_scalar(w4[:, 1], sa[:, 1], float(C), None, ALU.mult))
            v.tensor_tensor(w0, w0, ca1[:], ALU.mult)
            link(v.tensor_tensor(w3, w3, w4, ALU.add))
            v.scalar_tensor_tensor(score[:, 0, 0], w2[:, 0], float(C), w0[:, 0], ALU.mult, ALU.add)
            v.scalar_tensor_tensor(score[:, 1, 1], w2[:, 1], float(C), w0[:, 1], ALU.mult, ALU.add)
            v.tensor_tensor(w4[:, 0], w3[:, 0], ca1[:, 0], ALU.mult)
            link(v.tensor_tensor(w4[:, 1], w3[:, 1], sa[:, 0], ALU.mult))
            v.tensor_tensor(score[:, 0, 1], w4[:, 0], w4[:, 1], ALU.add)
            link(v.tensor_tensor(score[:, 1, 0], w4[:, 0], w4[:, 1], ALU.add))
            link(v.tensor_tensor(w0, score[:, :, 0], score[:, :, 1], ALU.max))
            for m in range(NB):
                ins = v.tensor_tensor(score[:, :, m], score[:, :, m], w0, ALU.subtract)
            link(ins)
            v.tensor_scalar(score[:], score[:], SCORE_SCALE, None, ALU.mult).then_inc(shifted, 1)
            dve.wait_ge(exp_done, 1)
            link(v.tensor_tensor(w0, prob[:, :, 0], prob[:, :, 1], ALU.add))
            link(v.reciprocal(w1, w0))
            for m in range(NB):
                ins = v.tensor_tensor(prob[:, :, m], prob[:, :, m], w1, ALU.mult)
            link(ins)
            ga = gate_a[:, 0]
            for n in range(NB):
                v.scalar_tensor_tensor(att[:, n, n], prob[:, n, n], 1.0, ga[:, n], ALU.add, ALU.mult)
                ins = v.tensor_tensor(att[:, n, 1 - n], prob[:, n, 1 - n], ga[:, n], ALU.mult)
            link(ins)
            for n in range(NB):
                v.tensor_tensor(coef[:, 0, n], att[:, n, n], ca1[:, n], ALU.mult)
                v.tensor_tensor(coef[:, 1, n], att[:, n, 1 - n], ca1[:, 1 - n], ALU.mult)
                v.tensor_tensor(w2[:, n], att[:, n, n], sa[:, n], ALU.mult)
                ins = v.tensor_tensor(w3[:, n], att[:, n, 1 - n], sa[:, 1 - n], ALU.mult)
            link(ins)
            v.tensor_tensor(coef[:, 2], w2, w3, ALU.add).then_inc(coef_ready, 1)
            dve.wait_ge(coef_ready, 1)

            def split_lo(p, ahead, e):
                _, _, size = kind_of(p % NSLOT)
                r = p % 2
                dve.wait_ge(hi_ready, e * NSLOT + ahead + (p + 1))
                v.tensor_tensor(w_lo[r][:, 0:size], w_raw[r][:, 0:size], w_hi[r][:, 0:size].bitcast(F32),
                                ALU.subtract).then_inc(lo_ready, 1)

            for k in range(KD):
                dve.wait_ge(u0_ready, k + 1)
                for n in range(NB):
                    ins = v.scalar_tensor_tensor(u_0[:, k, n, :], xhat_0[:, k, 1 - n, :], coef[:, 1, n, k:k + 1],
                                                 u_0[:, k, n, :], ALU.mult, ALU.add)
                link(ins)
                v.tensor_tensor(acc[:, k], u_0[:, k], x_0[:, k], ALU.add).then_inc(x20_ready, 1)
            dve.wait_ge(x20_ready, KD)
            v.nop().then_inc(next_free, 1)
            dve.wait_ge(mean20_mm, 1)
            for q in range(2):
                ks = slice(q * KD // 2, (q + 1) * KD // 2)
                v.scalar_tensor_tensor(tok(d_0)[:, ks], bc(ps_mean2, KD // 2), -1.0 / D, tok(acc)[:, ks], ALU.mult,
                                       ALU.add).then_inc(d20_ready, 1)
            take(3, ps_mod[1], ROWS[2], half, half + 2)
            link(v.tensor_scalar(cb1[:], mod[:, half + 1], 1.0, None, ALU.add))
            split_lo(0, 0, 0)
            dve.wait_ge(std20_ready, 1)
            link(v.reciprocal(rstd2, std2))

            def low(k):
                dve.wait_ge(xn_hi_ready, k + 1)
                for n in range(NB):
                    cols = slice(n * CC, (n + 1) * CC)
                    ins = v.scalar_tensor_tensor(xn_lo[:, k, cols], d_0[:, k, n, :], mod[:, 3, n, k:k + 1],
                                                 xn_hi[:, k, cols].bitcast(F32), ALU.add, ALU.subtract)
                ins.then_inc(xn_ready, 1)

            for k in range(KD):
                for n in range(NB):
                    ins = v.scalar_tensor_tensor(d_0[:, k, n, :], d_0[:, k, n, :], cb1[:, n, k:k + 1],
                                                 rstd2[:, n * CC:(n + 1) * CC], ALU.mult, ALU.mult)
                ins.then_inc(t20_ready, 1)
                if k:
                    low(k - 1)
            low(KD - 1)

            take(4, ps_mod[2], ROWS[3], half + 2, 2 * half)
            gate(1)

            dve.sem_inc(gu_bank_free, 2)
            dve.sem_inc(y_bank_free, 2)
            dve.sem_inc(h_ready, 1)
            dve.sem_inc(acc_ready, KD)

            split_lo(1, 0, 0)

            def chunk(e, last):
                def one(p, ahead):
                    kind, n, _ = kind_of(p)
                    if kind == "gu":
                        i = n if n < HALF0 else n - HALF0
                        tile = bass.ds(ahead + i, 1)
                        dve.wait_ge(silu_done, e * NGU + ahead + (n + 1))
                        dve.wait_ge(h_ready, e * NGU + ahead + (n + 1))
                        v.tensor_tensor(prod[:], ps_up[n % 2], sg[n % 2][:], ALU.mult).then_inc(gu_bank_free, 1)
                        dve.wait_ge(gu_bank_free, e * NGU + ahead + (n + 3))
                        v.tensor_scalar(h_hi[:, tile, :].rearrange("p o t -> p (o t)"), prod[:], 1.0, None,
                                        ALU.mult).then_inc(h_hi_done, 1)
                        dve.wait_ge(h_hi_done, e * NGU + ahead + (n + 1))
                        v.tensor_tensor(h_lo[:, tile, :].rearrange("p o t -> p (o t)"), prod[:],
                                        h_hi[:, tile, :].rearrange("p o t -> p (o t)").bitcast(F32),
                                        ALU.subtract).then_inc(h_ready, 1)
                    elif kind == "tail":
                        dve.wait_ge(silu_done, e * NGU + (n + 1))
                        dve.wait_ge(h_ready, e * NGU + (n + 1))
                        v.tensor_tensor(prod[0:TAIL, :], ps_gate[n % 2][TAIL:P, :], sg[n % 2][0:TAIL, :],
                                        ALU.mult).then_inc(gu_bank_free, 1)
                        dve.wait_ge(gu_bank_free, e * NGU + (n + 3))
                        v.tensor_scalar(h_hi[0:TAIL, HT - 1, :], prod[0:TAIL, :], 1.0, None, ALU.mult).then_inc(h_hi_done, 1)
                        dve.wait_ge(h_hi_done, e * NGU + (n + 1))
                        v.tensor_tensor(h_hi[TAIL:P, HT - 1, :], prod[0:TAIL, :], h_hi[0:TAIL, HT - 1, :].bitcast(F32),
                                        ALU.subtract).then_inc(h_ready, 1)
                    else:
                        m = n % KD
                        if n < KD:
                            dve.wait_ge(acc_ready, e * KD + KD)
                        dve.wait_ge(slot_done, e * NSLOT + ahead + (p + 1))
                        for b in range(NB):
                            tile = acc[:, bass.ds(ahead + m, 1), b, :].rearrange("p o c -> p (o c)")
                            ins = v.scalar_tensor_tensor(tile, ps_y[n % 2][:, b * CC:(b + 1) * CC],
                                                         gate_a[:, 1, b, bass.ds(ahead + m, 1)], tile, ALU.mult, ALU.add)
                        ins.then_inc(y_bank_free, 1)
                    if not (last and p + 2 >= NSLOT):
                        split_lo(p + 2, ahead, e)
                    if p == P_TAIL - 2 and not last:
                        dve.wait_ge(std2_ready, e + 1)
                        v.reciprocal(rstd2, std2).then_inc(rstd2_ready, 1)
                    if p == P_DN1 and not last:
                        for k in range(KD):
                            dve.wait_ge(xn_hi_ready, e * KD + (KD + k + 1))
                            v.tensor_tensor(xn_lo[:, k, :], tok(h_next)[:, k, :], xn_hi[:, k, :].bitcast(F32),
                                            ALU.subtract).then_inc(xn_ready, 1)
                steps(dve, one)

            with dve.Fori(0, NCH - 1) as e:
                chunk(e, False)
            chunk(NCH - 1, True)

        @block.tensor
        def _(pe):
            mm = nc.tensor.matmul
            pe.wait_ge(ones_ready, 1)
            pe.wait_ge(silu_ready, 1)
            pe.wait_ge(eye_loaded, 16)
            pe.sem_inc(mean_mm, 2)
            pe.sem_inc(sq_pair_used, 2)
            pe.sem_inc(sum_done, 1)

            def modulate(r, bank, j, group):
                rows, block, cols = ROWS[group], j // 2, slice(j % 2 * WPART, (j % 2 + 1) * WPART)
                start = max(ROWS) - NB - block * NB
                for k in range(KD):
                    ins = mm(bank[0:rows, cols], silu_pad[:, k, start:start + rows], wm[r][:, k, :],
                             start=j == k == 0, stop=j == GROUP[group] - 1 and k == KD - 1)
                ins.then_inc(mod_done, 1)

            def turn(group, bank, rows, at):
                pe.wait_ge(rows_copied, group + 1)
                n = ROWS[group]
                for c in range(NCOL):
                    ins = mm(bank[:, c * rows + at:c * rows + at + n], mod_rows[group % 2][0:n, c * P:(c + 1) * P],
                             eye_t[0:n, 0:n], start=True, stop=True)
                ins.then_inc(mod_ready, 1)

            with pe.Fori(0, NPAIR // 2) as t:
                def means(u, h):
                    i = 2 * u + h
                    pe.wait_ge(x_loaded[u][h], t * 16 + 16)
                    pe.wait_ge(mean_ready, t * 4 + (i + 1))
                    for k in range(PRE, KD):
                        mm(ps_mean[h], ones[:], tok(xbuf[u][:, h])[:, k, :], start=k == PRE, stop=False)
                    pe.wait_ge(presum_ready, t * 4 + (i + 1))
                    mm(ps_mean[h], ones[:], presum[:, h, :], start=False, stop=True).then_inc(mean_mm, 1)

                def variances(u, h):
                    i = 2 * u + h
                    pe.wait_ge(std_ready, t * 4 + (i + 1))
                    for j in range(SQ_PRE):
                        m = i * SQ_PRE + j
                        pe.wait_ge(sq_added, t * (4 * SQ_PRE) + (m + 2))
                        mm(ps_var[h], ones[:], sq_pair[:, m % 2, :], start=j == 0, stop=False).then_inc(sq_pair_used, 1)
                    pe.wait_ge(sq_ready, t * (4 * NSQ) + (i + 1) * NSQ)
                    mm(ps_var[h], ones[:], sq[:, 1, 0, :], start=False, stop=False)
                    mm(ps_var[h], ones[:], sq[:, 1, 1, :], start=False, stop=True).then_inc(sum_done, 1)

                def parts(first):
                    bank = ps[:, bass.ds(t + 4, 1), :].rearrange("p o c -> p (o c)")
                    for j in range(first, first + 2):
                        pe.wait_ge(wm_loaded[j % WM_RING], t * 32 + (16 * (j // WM_RING) + 16))
                        pe.sem_inc(pe_passed, 1)
                        modulate(j % WM_RING, bank, j, 0)

                means(0, 0)
                means(0, 1)
                means(1, 0)
                variances(0, 0)
                means(1, 1)
                parts(0)
                variances(0, 1)
                parts(2)
                variances(1, 0)
                variances(1, 1)
                parts(4)

            def parts(group, js):
                for j in js:
                    w = FIRST[group] + j
                    pe.wait_ge(wm_loaded[w % WM_RING], 16 * (w // WM_RING) + 16)
                    modulate(w % WM_RING, ps_rows[group], j, group)

            parts(2, range(GROUP[2] // 2))
            turn(0, ps_mod[0], ROWS[0] + ROWS[1], 0)
            turn(1, ps_mod[0], ROWS[0] + ROWS[1], ROWS[0])
            parts(2, range(GROUP[2] // 2, GROUP[2]))

            for k in range(KD):
                pe.wait_ge(x20_ready, k + 1)
                ins = mm(ps_mean2, ones[:], tok(acc)[:, k, :], start=k == 0, stop=k == KD - 1)
            ins.then_inc(mean20_mm, 1)
            turn(2, ps_mod[1], ROWS[2], 0)
            for j in range(NSQ):
                pe.wait_ge(sq20_ready, j + 1)
                for k in range(SQ_PER):
                    ins = mm(ps_var2, ones[:], sq[:, j % 2, k, :], start=j == k == 0, stop=j == NSQ - 1 and k == SQ_PER - 1)
                ins.then_inc(sq20_used, 1)
            parts(3, range(GROUP[3]))
            turn(3, ps_mod[2], ROWS[3], 0)

            def gate_up(p, ahead, e):
                kind, n, _ = kind_of(p)
                r = p % 2
                pe.wait_ge(lo_ready, e * NSLOT + ahead + (p + 1))
                pe.wait_ge(gu_bank_free, e * NGU + ahead + (n + 1))
                for j, bank in enumerate((ps_gate[n % 2], ps_up[n % 2]) if kind == "gu" else (ps_gate[n % 2],)):
                    for k in range(KD):
                        w = slice((j * KD + k) * P, (j * KD + k + 1) * P)
                        if p == 0 and j == 0:
                            pe.wait_ge(xn_ready, e * KD + (k + 1))
                        mm(bank, w_hi[r][:, w], xn_hi[:, k, :], start=k == 0, stop=False)
                        mm(bank, w_hi[r][:, w], xn_lo[:, k, :], start=False, stop=False)
                        ins = mm(bank, w_lo[r][:, w], xn_hi[:, k, :], start=False, stop=k == KD - 1)
                ins.then_inc(slot_done, 1)

            def down(p, ahead, e):
                _, n, _ = kind_of(p)
                half = n // KD
                r = p % 2
                bank = ps_y[n % 2]
                pe.wait_ge(lo_ready, e * NSLOT + ahead + (p + 1))
                pe.wait_ge(y_bank_free, e * NDN + ahead + (n + 1))
                known = HALF0 if half == 0 else NGU
                pe.wait_ge(h_ready, e * NGU + known)
                for k in range(HT):
                    w = slice(k * P, (k + 1) * P)
                    if k == HT - 1:
                        pe.wait_ge(h_ready, e * NGU + (known + 1))
                    if half == 1 and k == HT - 1:
                        mm(bank, w_hi[r][:, w], h_hi[:, k, :], start=False, stop=False)
                        ins = mm(bank, w_lo[r][:, w], h_hi[:, k, :], start=False, stop=True)
                    else:
                        mm(bank, w_hi[r][:, w], h_hi[:, k, :], start=k == 0, stop=False)
                        mm(bank, w_hi[r][:, w], h_lo[:, k, :], start=False, stop=False)
                        ins = mm(bank, w_lo[r][:, w], h_hi[:, k, :], start=False, stop=k == HT - 1)
                ins.then_inc(slot_done, 1)

            def loop(slot, first, n, e):
                with pe.Fori(0, n // 2) as i:
                    for u in range(2):
                        slot(first + u, 2 * i, e)
                if n % 2:
                    slot(first + n - 1, 0, e)

            def chunk(e, last):
                gate_up(0, 0, e)
                loop(gate_up, 1, HALF0 - 1, e)
                loop(down, P_DN0, KD, e)
                if not last:
                    pe.wait_ge(sum2_ready, e + 1)
                    mm(ps_mean2, ones[:], pool_acc, start=True, stop=True).then_inc(stat2_mm, 1)
                loop(gate_up, P_GU1, HALF1 - 1, e)
                if not last:
                    pe.wait_ge(sq2_ready, e + 1)
                    mm(ps_var2, ones[:], pool_acc, start=True, stop=True).then_inc(stat2_mm, 1)
                gate_up(P_TAIL - 1, 0, e)
                gate_up(P_TAIL, 0, e)
                loop(down, P_DN1, KD, e)

            with pe.Fori(0, NCH - 1) as e:
                chunk(e, False)
            chunk(NCH - 1, True)


def chunks_of(a):
    return np.ascontiguousarray(a.reshape(NB, NCH, CC, KD, P).transpose(1, 4, 3, 0, 2)).reshape(NCH, P, KD * T)


def tiles_of(w, n):
    return w.reshape(n, KD, P).transpose(2, 1, 0)


def kernel(L0_attn_x, L0_ffn_W_gate, L0_ffn_W_up, L0_ffn_W_down, L0_c, L0_wmod):
    import concourse.bacc as bacc
    from concourse.bass_utils import run_bass_kernel_spmd

    xin, wg, wu, wd, c, wmod = (np.asarray(a) for a in (L0_attn_x, L0_ffn_W_gate, L0_ffn_W_up, L0_ffn_W_down, L0_c, L0_wmod))
    whole = FT * P
    gu = np.stack([np.stack([tiles_of(w[f * P:(f + 1) * P], P) for w in (wg, wu)], 1) for f in range(FT)])
    gut = np.concatenate([tiles_of(wg[whole:], TAIL), tiles_of(wu[whole:], TAIL)], 2)
    wdt = wd.T
    blocks = [wdt[f * P:(f + 1) * P] for f in range(FT)] + [np.concatenate([wdt[whole:], wdt[whole:]], 0)]
    halves = [np.stack(blocks[:HALF0]), np.stack(blocks[HALF0:])]
    dn = np.stack([h.reshape(HT, P, KD, P).transpose(2, 1, 0, 3) for h in halves])
    arrays = {
        "x": chunks_of(xin),
        "wgu": np.ascontiguousarray(gu).reshape(FT, P, GU),
        "wgut": np.ascontiguousarray(gut).reshape(1, P, GUT),
        "wdn": np.ascontiguousarray(dn).reshape(NDN, P, DN),
        "cT": np.ascontiguousarray(c.reshape(NB, KD, P).transpose(2, 1, 0)),
        "eye": np.eye(max(ROWS), dtype=np.float32),
        "wmod": np.ascontiguousarray(wmod.reshape(KD, P, NPART, WPART).transpose(2, 1, 0, 3)),
    }
    nc = bacc.Bacc("TRN2", target_bir_lowering=False, num_devices=1)
    args = [nc.dram_tensor(n, a.shape, mybir.dt.from_np(a.dtype), kind="ExternalInput").ap() for n, a in arrays.items()]
    out = nc.dram_tensor("out", (NCH, P, KD * T), F32, kind="ExternalOutput").ap()
    build(nc, *args, out)
    r = run_bass_kernel_spmd(nc, [arrays], core_ids=[0])
    y = r.results[0]["out"].reshape(NCH, P, KD, NB, CC)
    return np.ascontiguousarray(y.transpose(3, 0, 4, 2, 1)).reshape(NB, C, D)
```

```python
import numpy as np

import concourse.bass as bass
from concourse import mybir
from concourse.alu_op_type import AluOpType as ALU

F32 = mybir.dt.float32
F32R = mybir.dt.float32r
ACT = mybir.ActivationFunctionType

P = 128
NB = 2
D = 1024
C = 2048
F = 2752
KD = D // P
CC = 256
T = NB * CC
NCH = C // CC
NPAIR = NCH // 2
NMOD = 6
FT = F // P
TAIL = F - FT * P
assert 2 * TAIL == P
HALF0 = (FT + 1) // 2
HALF1 = FT - HALF0
HT = HALF0
assert HALF1 + 1 == HT
GU = 2 * KD * P
GUT = KD * P
DN = HT * P
NGU = FT + 1
NDN = 2 * KD
NSLOT = NGU + NDN
P_DN0 = HALF0
P_GU1 = P_DN0 + KD
P_TAIL = P_GU1 + HALF1
P_DN1 = P_TAIL + 1
assert NSLOT == P_DN1 + KD and NSLOT % 2 == 0 and NGU % 2 == 0
WPART = 256
NPART = NMOD * D // WPART
WM_RING = 3
BLOCK = 512
NCOL = BLOCK // P
GROUP = [6, 6, 8, 4]
FIRST = [sum(GROUP[:i]) for i in range(len(GROUP))]
ROWS = [n * WPART // BLOCK * NB for n in GROUP]
SQ_PER = 2
NSQ = KD // SQ_PER
PRE = (4, 6)
X2_POOL = 5
assert NPAIR == 4 and sum(GROUP) == NPART and 2 * WPART == BLOCK and GROUP[0] == GROUP[1] == 2 * WM_RING
EPS = 1e-5
GATE_MIN = 0.25
SCORE_SCALE = float(np.float32(1.0) / np.sqrt(np.float32(C)))


def build(nc, x, wgu, wgut, wdn, cT, eye, wmod, out):
    base = (nc.sbuf_base + 63) // 64 * 64
    K = 1024

    def sb(name, shape, dt, at):
        return nc.alloc_sbuf_tensor_at(name, [P] + shape, dt, offset=base + at)

    xbuf = [sb("xbuf0", [2, KD, NB, CC], F32, 32 * K), sb("xbuf1", [2, KD, NB, CC], F32, 64 * K)]
    dbuf = [sb("dbuf0", [2, KD, NB, CC], F32, 96 * K), sb("dbuf1", [2, KD, NB, CC], F32, 0)]
    x2_next = sb("x2_next", [KD, NB, CC], F32, 0)
    h_next = sb("h_next", [KD, NB, CC], F32, 16 * K)
    h_hi = sb("h_hi", [HT, T], F32R, 32 * K)
    h_lo = sb("h_lo", [HT, T], F32R, 54 * K)
    xn_hi = sb("xn_hi", [KD, T], F32R, 76 * K)
    xn_lo = sb("xn_lo", [KD, T], F32R, 92 * K)
    acc = sb("acc", [KD, NB, CC], F32, 108 * K)
    w_hi = [sb(f"w_hi{r}", [GU], F32R, (124 + 24 * r) * K) for r in range(2)]
    w_lo = [sb(f"w_lo{r}", [GU], F32R, (132 + 24 * r) * K) for r in range(2)]
    w_raw = [sb(f"w_raw{r}", [GU], F32, (140 + 24 * r) * K) for r in range(2)]
    mean = sb("mean", [2, 2, T], F32, 128 * K)
    rows_first = sb("rows_first", [2, BLOCK], F32, 140 * K)
    sq_pair = sb("sq_pair", [2, T], F32, 136 * K)
    wm = [sb(f"wm{r}", [KD, WPART], F32, (148 + 8 * r) * K) for r in range(WM_RING)]
    sq = sb("sq", [2, SQ_PER, T], F32, 172 * K)
    sg = [sb(f"sg{r}", [T], F32, (172 + 2 * r) * K) for r in range(2)]
    prod = sb("prod", [T], F32, 176 * K)
    SMALL = 180 * K
    at = [SMALL]

    def small(name, shape, dt=F32):
        size = int(np.prod(shape)) * 4
        t = sb(name, shape, dt, at[0])
        at[0] += (size + 31) // 32 * 32
        return t

    presum = small("presum", [2, T])
    presums = [presum, sb("presum1", [2, T], F32, 144 * K)]
    rstd = small("rstd", [2, 2, T])
    std = small("std", [2, T])
    junk_a = small("junk_a", [2, 2, CC])
    junk_v = small("junk_v", [2, 2, CC])
    ones = small("ones", [P])
    ones_r = small("ones_r", [P], F32R)
    eye_t = small("eye_t", [max(ROWS)])
    ct = small("ct", [KD, NB])
    silu_pad = small("silu_pad", [KD, 2 * max(ROWS) - NB])
    eps_pair = small("eps_pair", [2])
    eps_t, eps_root = eps_pair[:, 0:1], eps_pair[:, 1:2]
    part = small("part", [2, 5, KD])
    sums = small("sums", [2, 5, KD])
    xs = small("xs", [5, KD])
    mod = small("mod", [NMOD, NB, KD])
    ca1 = small("ca1", [NB, KD])
    cb1 = small("cb1", [NB, KD])
    gate_a = small("gate_a", [2, NB, KD])
    gate_t = small("gate_t", [2, NB, KD])
    score = small("score", [NB, NB, KD])
    prob = small("prob", [NB, NB, KD])
    tmp = [small(f"tmp{i}", [NB, KD]) for i in range(5)]
    att = score
    coef = small("coef", [3, NB, KD])
    mod_rows = [rows_first[:, 0, :], rows_first[:, 1, :], presum[:, 0, :], presum[:, 1, :]]
    pool_u, pool_v = presum[:, 0, :], presum[:, 1, :]
    pool_acc, pool_sq = std[:, 0, :], std[:, 1, :]
    sum_hi, sum_lo = sb("sum_hi", [T], F32R, SMALL), sb("sum_lo", [T], F32R, SMALL + T * 4)
    stat1 = junk_a[:].rearrange("p r h c -> p r (h c)")
    mean2, std2, rstd2 = rstd[:, 0, 0, :], rstd[:, 0, 1, :], rstd[:, 1, 0, :]
    x_0, xhat_0, u_0, d_0 = xbuf[1][:, 0], dbuf[1][:, 0], xbuf[0][:, 0], xbuf[0][:, 1]

    assert base + at[0] <= nc.sbuf_usable_end, (base + at[0], nc.sbuf_usable_end)
    ps = nc.alloc_psum_tensor("ps", [P, 8, T], F32)
    ps_mean, ps_var = [[ps[:, 0, :], ps[:, 1, :]], [ps[:, 2, :], ps[:, 3, :]]], [ps[:, 6, :], ps[:, 7, :]]
    ROWS_BANK = 4
    ps_rows = [ps[:, ROWS_BANK, :], ps[:, ROWS_BANK + 1, :], ps[:, 3, :], ps[:, 5, :]]
    ps_mod = [ps[:, 2, :], ps[:, 4, :], ps[:, 7, :]]
    ps_gate, ps_up, ps_y = [ps[:, 0, :], ps[:, 1, :]], [ps[:, 2, :], ps[:, 3, :]], [ps[:, 4, :], ps[:, 5, :]]
    ps_mean2, ps_var2 = ps[:, 6, :], ps[:, 7, :]

    stats_dram = nc.dram_tensor("stats", [NCH, 2, T], F32, kind="Internal").ap()

    sem = nc.alloc_semaphore
    c_loaded, eye_loaded, eps_ready, ones_ready = sem("c_loaded"), sem("eye_loaded"), sem("eps_ready"), sem("ones_ready")
    x_loaded = [[sem(f"x_loaded{u}{h}") for h in range(2)] for u in range(2)]
    presum_ready, mean_mm, mean_ready = sem("presum_ready"), sem("mean_mm"), sem("mean_ready")
    centred, sq_ready, sq_added = sem("centred"), sem("sq_ready"), sem("sq_added")
    sq_pair_used = sem("sq_pair_used")
    std_ready, rstd_ready = sem("std_ready"), sem("rstd_ready")
    mean_saved, rstd_saved = ([sem(f"{w}_saved{u}") for u in range(2)] for w in ("mean", "rstd"))
    xhat_ready, sqsum_done, cross_done = sem("xhat_ready"), sem("sqsum_done"), sem("cross_done")
    wm_loaded = [sem(f"wm_loaded{r}") for r in range(WM_RING)]
    silu_zeroed, silu_ready, mod_done = sem("silu_zeroed"), sem("silu_ready"), sem("mod_done")
    rows_copied, mod_ready = sem("rows_copied"), sem("mod_ready")
    sums_ready = sem("sums_ready")
    shifted, exp_done, coef_ready = sem("shifted"), sem("exp_done"), sem("coef_ready")
    u0_ready, v20_ready, x20_pool, x20_ready, d20_ready, t20_ready = (
        sem("u0_ready"), sem("v20_ready"), sem("x20_pool"), sem("x20_ready"), sem("d20_ready"), sem("t20_ready"))
    dve_chain, pool_chain, pool_passed = sem("dve_chain"), sem("pool_chain"), sem("pool_passed")
    act_passed = sem("act_passed")
    raw_loaded = [sem(f"raw_loaded{r}") for r in range(2)]
    hi_ready, lo_ready, slot_done = sem("hi_ready"), sem("lo_ready"), sem("slot_done")
    gu_bank_free, y_bank_free = sem("gu_bank_free"), sem("y_bank_free")
    silu_done, h_hi_done, h_ready = sem("silu_done"), sem("h_hi_done"), sem("h_ready")
    xn_hi_ready, xn_ready = sem("xn_hi_ready"), sem("xn_ready")
    next_free, next_x, next_stat = sem("next_free"), sem("next_x"), sem("next_stat")
    acc_ready, out_stored = sem("acc_ready"), sem("out_stored")
    sum2_ready, sq2_ready, stat2_mm = sem("sum2_ready"), sem("sq2_ready"), sem("stat2_mm")
    ones_r_ready, sum_hi_ready, sum_lo_ready = sem("ones_r_ready"), sem("sum_hi_ready"), sem("sum_lo_ready")
    sq20_ready, sq20_used, mean20_mm, std20_ready = sem("sq20_ready"), sem("sq20_used"), sem("mean20_mm"), sem("std20_ready")
    mean2_ready, std2_ready, rstd2_ready, h_next_ready = (
        sem("mean2_ready"), sem("std2_ready"), sem("rstd2_ready"), sem("h_next_ready"))

    def bc(ap, n):
        return ap[:, None, :].broadcast_to([P, n, T])

    def tok(ap):
        return ap.rearrange("p k b c -> p k (b c)")

    def kind_of(p):
        if p < P_DN0:
            return "gu", p, GU
        if p < P_GU1:
            return "dn", p - P_DN0, DN
        if p < P_TAIL:
            return "gu", p - KD, GU
        if p == P_TAIL:
            return "tail", FT, GUT
        return "dn", p - P_DN1 + KD, DN

    STEPS = []
    for first, end in ((0, 2), (2, P_DN0), (P_DN0, P_GU1), (P_GU1, P_TAIL), (P_TAIL, P_DN1), (P_DN1, P_DN1 + 1), (P_DN1 + 1, NSLOT)):
        n = max(0, (end - first - 2) // 2)
        if n:
            STEPS.append((first, n, 2))
        STEPS += [(p, 1, 1) for p in range(first + 2 * n, end)]

    def steps(eng, one):
        for first, n, per in STEPS:
            if n > 1:
                with eng.Fori(0, n) as i:
                    for u in range(per):
                        one(first + u, 2 * i)
            else:
                one(first, 0)

    block = nc.Block()
    with block as block:

        @block.sync
        def _(sp):
            def load_part(w):
                if w >= WM_RING:
                    sp.wait_ge(mod_done, w - WM_RING + 1)
                sp.dma_start(wm[w % WM_RING][:], wmod[w]).then_inc(wm_loaded[w % WM_RING], 16)

            def load_pair(a):
                if a >= 2:
                    sp.wait_ge(centred, 4 * (a - 1))
                chunk = 2 * ((a + 1) % NPAIR)
                for h in range(2):
                    sp.dma_start(tok(xbuf[a % 2][:, h]), x[chunk + h].rearrange("p (k t) -> p k t", k=KD)).then_inc(
                        x_loaded[a % 2][h], 16)

            sp.dma_start(ct[:], cT).then_inc(c_loaded, 16)
            load_pair(0)
            sp.dma_start(eye_t[0:max(ROWS), :], eye).then_inc(eye_loaded, 16)
            load_pair(1)
            for w in range(WM_RING):
                load_part(w)
            load_pair(2)
            load_pair(3)

            def load_slot(p, ahead, e):
                kind, n, size = kind_of(p % NSLOT)
                r = p % 2
                if not (isinstance(e, int) and e == 0 and isinstance(ahead, int) and p < 2):
                    sp.wait_ge(lo_ready, e * NSLOT + ahead + (p - 1))
                if kind == "gu":
                    src = wgu[bass.ds(ahead + n, 1), :, :]
                elif kind == "tail":
                    src = wgut[0:1, :, :]
                else:
                    src = wdn[bass.ds(ahead + n, 1), :, :]
                sp.dma_start(w_raw[r][:, 0:size], src.rearrange("o p w -> (o p) w")).then_inc(raw_loaded[r], 16)

            for w in range(WM_RING, FIRST[3]):
                load_part(w)
            sp.wait_ge(mod_ready, 2)
            load_slot(0, 0, 0)
            for w in range(FIRST[3], NPART):
                load_part(w)
            sp.wait_ge(mod_done, NPART)
            load_slot(1, 0, 0)
            for u in range(2):
                sp.wait_ge(mean_saved[u], 16 + 16 * (NPAIR // 2))
                sp.wait_ge(rstd_saved[u], 16 + 16 * (NPAIR // 2))

            def store(p, ahead, e):
                m = p - P_DN1
                sp.wait_ge(y_bank_free, e * NDN + ahead + (2 + KD + m + 1))
                sp.dma_start(out[bass.ds(e, 1), :, bass.ds((ahead + m) * T, T)].rearrange("o p t -> (o p) t"),
                             acc[:, bass.ds(ahead + m, 1), :, :].rearrange("p o b c -> p (o b c)")).then_inc(out_stored, 16)

            def chunk(e, last):
                def one(p, ahead):
                    if not (last and p + 2 >= NSLOT):
                        load_slot(p + 2, ahead, e)
                    if p > P_DN1:
                        store(p - 1, ahead, e)
                    if p == 1 and not last:
                        sp.wait_ge(next_free, e + 1)
                        sp.dma_start(x2_next[:].rearrange("p k b c -> p (k b c)"),
                                     x[bass.ds(e + 1, 1), :, :].rearrange("o p w -> (o p) w")).then_inc(next_x, 16)
                        sp.dma_start(stat1.rearrange("p s t -> p (s t)"),
                                     stats_dram[bass.ds(e + 1, 1), :, :].rearrange("o s t -> o (s t)").broadcast_to(
                                         [P, 2 * T])).then_inc(next_stat, 16)
                steps(sp, one)
                store(NSLOT - 1, 0, e)

            with sp.Fori(0, NCH - 1) as e:
                chunk(e, False)
            chunk(NCH - 1, True)
            sp.wait_ge(out_stored, 16 * KD * NCH)

        @block.gpsimd
        def _(pool):
            g = nc.gpsimd
            g.memset(ones[:], 1.0).then_inc(ones_ready, 1)
            g.memset(silu_pad[:], 0.0).then_inc(silu_zeroed, 1)
            pool.sem_inc(sq_added, 2)

            links = [0]
            for t in range(NPAIR // 2):
                def sum_tiles(u, h):
                    i = 2 * u + h
                    pool.wait_ge(x_loaded[u][h], t * 16 + 16)
                    pool.wait_ge(mean_mm, t * 4 + (i + 1))
                    xk, to = tok(xbuf[u][:, h]), presums[u][:, h, :]
                    for k in range(1, PRE[t]):
                        ins = g.tensor_tensor(to, xk[:, 0, :] if k == 1 else to, xk[:, k, :], ALU.add)
                        if k < PRE[t] - 1:
                            ins.then_inc(pool_chain, 1)
                            links[0] += 1
                            pool.wait_ge(pool_chain, links[0])
                        else:
                            ins.then_inc(presum_ready, 1)

                def add_squares(u, h):
                    i = 2 * u + h
                    for j in range(NSQ):
                        n = i * NSQ + j
                        pool.wait_ge(sq_ready, t * (4 * NSQ) + (n + 1))
                        pool.wait_ge(sq_pair_used, t * (4 * NSQ) + (n + 1))
                        g.tensor_tensor(sq_pair[:, j % 2, :], sq[:, j % 2, 0, :], sq[:, j % 2, 1, :], ALU.add).then_inc(
                            sq_added, 1)

                sum_tiles(0, 0)
                sum_tiles(0, 1)
                sum_tiles(1, 0)
                if t == 0:
                    add_squares(0, 0)
                    sum_tiles(1, 1)
                else:
                    sum_tiles(1, 1)
                    add_squares(0, 0)
                add_squares(0, 1)
                add_squares(1, 0)
                add_squares(1, 1)

            for k in range(X2_POOL):
                pool.wait_ge(v20_ready, k + 1)
                g.tensor_tensor(tok(acc)[:, k, :], tok(u_0)[:, k, :], tok(x_0)[:, k, :], ALU.add).then_inc(x20_pool, 1)

            chain0 = links[0]

            def chunk(e, first):
                count = [0]
                total = chunk_links

                def pause(sem_, value):
                    pool.wait_ge(sem_, value)
                    pool.sem_inc(pool_passed, 1)

                def link(ins):
                    ins.then_inc(pool_chain, 1)
                    count[0] += 1
                    pause(pool_chain, e * total + (chain0 + count[0]))

                if not first:
                    pause(out_stored, e * (16 * KD))
                    for k in range(KD):
                        ins = g.tensor_copy(tok(acc)[:, k, :], tok(x2_next)[:, k, :])
                        if k < KD - 1:
                            ins.then_inc(acc_ready, 1)
                    link(ins)
                    pool.nop().then_inc(acc_ready, 1)
                    pool.nop().then_inc(next_free, 1)
                pool.wait_ge(next_x, e * 16 + 16)
                pool.wait_ge(next_stat, e * 16 + 16)
                pool.wait_ge(xn_ready, e * KD + KD)
                if not first:
                    pause(stat2_mm, e * 2)
                hk, xk = tok(h_next), tok(x2_next)
                for k in range(KD):
                    link(g.tensor_tensor(hk[:, k, :], xk[:, k, :], stat1[:, 0, :], ALU.subtract))
                    link(g.tensor_tensor(hk[:, k, :], hk[:, k, :], stat1[:, 1, :], ALU.mult))
                    for n in range(NB):
                        cols = slice(n * CC, (n + 1) * CC)
                        g.tensor_scalar(pool_u[:, cols], h_next[:, k, n, :], coef[:, 0, n, k:k + 1],
                                        coef[:, 2, n, k:k + 1], ALU.mult, ALU.add)
                        ins = g.tensor_scalar(pool_v[:, cols], h_next[:, k, 1 - n, :], coef[:, 1, n, k:k + 1], 0.0,
                                              ALU.mult, ALU.add)
                    link(ins)
                    link(g.tensor_tensor(pool_u, pool_u, pool_v, ALU.add))
                    link(g.tensor_tensor(xk[:, k, :], xk[:, k, :], pool_u, ALU.add))
                    if k == 0:
                        link(g.tensor_copy(pool_acc, xk[:, 0, :]))
                    elif k < KD - 1:
                        link(g.tensor_tensor(pool_acc, pool_acc, xk[:, k, :], ALU.add))
                    else:
                        g.tensor_tensor(pool_acc, pool_acc, xk[:, k, :], ALU.add).then_inc(sum2_ready, 1)
                pool.wait_ge(mean2_ready, e + 1)
                for k in range(KD):
                    link(g.tensor_tensor(hk[:, k, :], xk[:, k, :], mean2, ALU.subtract))
                    if k == 0:
                        link(g.tensor_tensor(pool_acc, hk[:, 0, :], hk[:, 0, :], ALU.mult))
                    else:
                        link(g.tensor_tensor(pool_sq, hk[:, k, :], hk[:, k, :], ALU.mult))
                        ins = g.tensor_tensor(pool_acc, pool_acc, pool_sq, ALU.add)
                        if k < KD - 1:
                            link(ins)
                        else:
                            ins.then_inc(sq2_ready, 1)
                pool.wait_ge(rstd2_ready, e + 1)
                for k in range(KD):
                    link(g.tensor_tensor(hk[:, k, :], hk[:, k, :], rstd2, ALU.mult))
                    for n in range(NB):
                        ins = g.tensor_scalar(h_next[:, k, n, :], h_next[:, k, n, :], cb1[:, n, k:k + 1],
                                              mod[:, 3, n, k:k + 1], ALU.mult, ALU.add)
                    link(ins)
                pool.nop().then_inc(h_next_ready, 1)
                return count[0]

            chunk_links = (6 * KD - 1) + (3 * KD - 2) + 2 * KD + 1
            pool.wait_ge(coef_ready, 1)
            assert chunk(0, True) == chunk_links - 1
            chain0 -= 1
            with pool.Fori(1, NCH - 1) as e:
                n = chunk(e, False)
            assert n == chunk_links
            pool.wait_ge(out_stored, (NCH - 1) * 16 * KD)
            for k in range(KD):
                g.tensor_copy(tok(acc)[:, k, :], tok(x2_next)[:, k, :]).then_inc(acc_ready, 1)

        @block.scalar
        def _(act):
            s = nc.scalar
            act.wait_ge(c_loaded, 16)
            act.wait_ge(silu_zeroed, 1)
            s.activation(silu_pad[:, :, max(ROWS) - NB:max(ROWS)], ct[:], ACT.Silu).then_inc(silu_ready, 1)
            act.wait_ge(eps_ready, 1)

            for u in range(2):
                act.sem_inc(mean_saved[u], 16)
                act.sem_inc(rstd_saved[u], 16)
            act.sem_inc(mean_ready, 4)
            act.sem_inc(std_ready, 2)
            act.sem_inc(sqsum_done, 4 * KD)

            with act.Fori(0, NPAIR // 2) as t:
                def copy_mean(u, h):
                    i = 2 * u + h
                    act.wait_ge(centred, t * 8 + 2 * (i + 1))
                    act.wait_ge(mean_saved[u], t * 16 + 16)
                    s.mul(mean[0:1, u, h, :], ps_mean[u][h][0:1, :], 1.0 / D).then_inc(mean_ready, 1)

                def save(u, which, rows, ready, credit, saved):
                    act.wait_ge(ready, t * 4 + (2 * u + 2 + credit))
                    chunk = t * 4 + 2 if u == 0 else t * -4 + 4
                    s.dma_start(stats_dram[bass.ds(chunk, 2), which, :].rearrange("(o h) t -> o h t", o=1),
                                rows[0:1, u]).then_inc(saved[u], 16)

                def square(u, h, js):
                    i = 2 * u + h
                    for j in js:
                        act.wait_ge(centred, t * 8 + (2 * i + j * 2 // NSQ + 1))
                        act.wait_ge(sq_added, t * (4 * NSQ) + (i * NSQ + j + 1))
                        s.activation(sq[:, j % 2], tok(dbuf[u][:, h])[:, j * SQ_PER:(j + 1) * SQ_PER, :], ACT.Square).then_inc(
                            sq_ready, 1)

                def root(u, h):
                    i = 2 * u + h
                    act.wait_ge(sq_pair_used, t * (4 * NSQ) + (i * NSQ + NSQ + 2))
                    act.wait_ge(rstd_ready, t * 4 + (i + 1))
                    s.activation(std[:, h, :], ps_var[h], ACT.Sqrt, bias=eps_t, scale=1.0 / D).then_inc(std_ready, 1)

                def square_sums(u, ks):
                    for k in ks:
                        for b in range(NB):
                            n = 2 * u * KD + NB * k + b
                            act.wait_ge(xhat_ready, t * (4 * KD) + (n + 1))
                            act.wait_ge(sqsum_done, t * (4 * KD) + (4 * KD + n - 1))
                            s.activation(junk_a[:, b], dbuf[u][:, :, k, b, :], ACT.Square,
                                         accum_out=part[:, u, 2 + b, k:k + 1]).then_inc(sqsum_done, 1)

                def copy_first_rows():
                    act.wait_ge(mod_done, t * GROUP[0] + GROUP[0])
                    act.sem_inc(act_passed, 1)
                    s.copy(rows_first[0:ROWS[0], bass.ds(t, 1), :], ps[0:ROWS[0], bass.ds(t + ROWS_BANK, 1), :]).then_inc(
                        rows_copied, 1)

                for u, h in ((0, 0), (0, 1), (1, 0), (1, 1)):
                    square(u, h, range(NSQ // 2))
                    if (u, h) != (0, 0):
                        root(u if h else 0, 1 - h)
                    square(u, h, range(NSQ // 2, NSQ))
                    copy_mean(u, h)
                    if h:
                        save(u, 0, mean, mean_ready, 4, mean_saved)
                root(1, 1)
                save(0, 1, rstd, rstd_ready, 2, rstd_saved)
                square_sums(0, range(KD))
                save(1, 1, rstd, rstd_ready, 2, rstd_saved)
                square_sums(1, range(KD // 2))
                copy_first_rows()
                square_sums(1, range(KD // 2, KD))

            def copy_rows(i):
                act.wait_ge(mod_done, FIRST[i] + GROUP[i])
                s.copy(mod_rows[i][0:ROWS[i], :], ps_rows[i][0:ROWS[i], :]).then_inc(rows_copied, 1)

            act.wait_ge(shifted, 1)
            s.activation(prob[:], score[:], ACT.Exp).then_inc(exp_done, 1)

            def split_hi(p, ahead, e):
                _, _, size = kind_of(p % NSLOT)
                r = p % 2
                act.wait_ge(raw_loaded[r], e * (8 * NSLOT) + 8 * ahead + (16 * (p // 2) + 16))
                if p >= 2:
                    act.wait_ge(slot_done, e * NSLOT + ahead + (p - 1))
                s.copy(w_hi[r][:, 0:size], w_raw[r][:, 0:size]).then_inc(hi_ready, 1)

            act.wait_ge(coef_ready, 1)
            for k in range(KD):
                for n in range(NB):
                    ins = s.activation(u_0[:, k, n, :], xhat_0[:, k, n, :], ACT.Identity,
                                       bias=coef[:, 2, n, k:k + 1], scale=coef[:, 0, n, k:k + 1])
                ins.then_inc(u0_ready, 1)
            for u in range(2):
                act.wait_ge(mean_saved[u], 16 + 16 * (NPAIR // 2))
                act.wait_ge(rstd_saved[u], 16 + 16 * (NPAIR // 2))
            split_hi(0, 0, 0)
            copy_rows(2)
            s.activation(eps_root, eps_t, ACT.Sqrt)
            for j in range(NSQ):
                act.wait_ge(d20_ready, j + 1)
                if j >= 2:
                    act.wait_ge(sq20_used, j - 1)
                s.activation(sq[:, j % 2], tok(d_0)[:, j * SQ_PER:(j + 1) * SQ_PER, :], ACT.Square).then_inc(sq20_ready, 1)
            act.wait_ge(sq20_used, NSQ)
            s.activation(std2, ps_var2, ACT.Sqrt, bias=eps_t, scale=1.0 / D).then_inc(std20_ready, 1)

            for k in range(KD):
                act.wait_ge(t20_ready, k + 1)
                for n in range(NB):
                    ins = s.activation(xn_hi[:, k, n * CC:(n + 1) * CC], u_0[:, k, n, :], ACT.Identity,
                                       bias=mod[:, 3, n, k:k + 1])
                ins.then_inc(xn_hi_ready, 1)
                if k == 1:
                    copy_rows(3)
            split_hi(1, 0, 0)

            def chunk(e, last):
                def one(p, ahead):
                    kind, n, _ = kind_of(p)
                    if kind != "dn":
                        rows = P if kind == "gu" else TAIL
                        act.wait_ge(slot_done, e * NSLOT + ahead + (p + 1))
                        act.wait_ge(gu_bank_free, e * NGU + ahead + (n + 1))
                        s.activation(sg[n % 2][0:rows, :], ps_gate[n % 2][0:rows, :], ACT.Silu).then_inc(silu_done, 1)
                    if not (last and p + 2 >= NSLOT):
                        split_hi(p + 2, ahead, e)
                    if p == P_GU1 - 2 and not last:
                        act.wait_ge(sum2_ready, e + 1)
                        s.copy(sum_hi[:], pool_acc).then_inc(sum_hi_ready, 1)
                    if p == P_TAIL - 2 and not last:
                        act.wait_ge(sq2_ready, e + 1)
                        s.copy(sum_hi[:], pool_acc).then_inc(sum_hi_ready, 1)
                    if p == P_GU1 - 1 and not last:
                        act.wait_ge(stat2_mm, e * 2 + 1)
                        s.mul(mean2, ps_mean2, 1.0 / D).then_inc(mean2_ready, 1)
                    if p == P_TAIL - 1 and not last:
                        act.wait_ge(stat2_mm, e * 2 + 2)
                        s.activation(std2, ps_var2, ACT.Sqrt, bias=eps_t, scale=1.0 / D).then_inc(std2_ready, 1)
                    if p == NSLOT - 3 and not last:
                        act.wait_ge(h_next_ready, e + 1)
                        for k in range(KD):
                            s.copy(xn_hi[:, k, :], tok(h_next)[:, k, :]).then_inc(xn_hi_ready, 1)
                steps(act, one)

            with act.Fori(0, NCH - 1) as e:
                chunk(e, False)
            chunk(NCH - 1, True)

        @block.vector
        def _(dve):
            v = nc.vector
            v.memset(eps_t, EPS).then_inc(eps_ready, 1)
            v.memset(sums[:], 0.0).then_inc(sums_ready, 1)
            v.memset(part[:], 0.0).then_inc(sums_ready, 1)
            dve.sem_inc(rstd_ready, 2)
            dve.sem_inc(cross_done, 2 * KD)
            dve.wait_ge(ones_ready, 1)
            v.tensor_copy(ones_r[:], ones[:]).then_inc(ones_r_ready, 1)
            dve.wait_ge(sums_ready, 2)

            with dve.Fori(0, NPAIR // 2) as t:
                def centre(u, h):
                    i = 2 * u + h
                    dve.wait_ge(mean_mm, t * 4 + (i + 5))
                    dve.wait_ge(sqsum_done, t * (4 * KD) + 2 * KD * (u + 1))
                    dve.wait_ge(cross_done, t * (2 * KD) + KD * (u + 1))
                    for q in range(2):
                        ks = slice(q * KD // 2, (q + 1) * KD // 2)
                        v.scalar_tensor_tensor(tok(dbuf[u][:, h])[:, ks], bc(ps_mean[u][h], KD // 2), -1.0 / D,
                                               tok(xbuf[u][:, h])[:, ks], ALU.mult, ALU.add).then_inc(centred, 1)

                def invert(u, h):
                    dve.wait_ge(std_ready, t * 4 + (2 * u + h + 3))
                    dve.wait_ge(rstd_saved[u], t * 16 + 16)
                    v.reciprocal(rstd[:, u, h, :], std[:, h, :]).then_inc(rstd_ready, 1)

                def normalise(u, k):
                    for b in range(NB):
                        v.scalar_tensor_tensor(dbuf[u][:, :, k, b, :], dbuf[u][:, :, k, b, :], 1.0,
                                               rstd[:, u, :, b * CC:(b + 1) * CC], ALU.mult, ALU.mult,
                                               accum_out=part[:, u, b, k:k + 1]).then_inc(xhat_ready, 1)

                def cross(u, k):
                    n = KD * u + k
                    dve.wait_ge(xhat_ready, t * (4 * KD) + NB * (n + 1))
                    dve.wait_ge(cross_done, t * (2 * KD) + (2 * KD + n - 1))
                    v.tensor_tensor_reduce(junk_v[:, k % 2], dbuf[u][:, :, k, 0, :], dbuf[u][:, :, k, 1, :], 1.0, 0.0, ALU.mult,
                                           ALU.add, accum_out=part[:, u, 4, k:k + 1]).then_inc(cross_done, 1)

                centre(0, 0)
                centre(0, 1)
                centre(1, 0)
                invert(0, 0)
                centre(1, 1)
                invert(0, 1)
                dve.wait_ge(sums_ready, t + 2)
                v.tensor_tensor(sums[:], sums[:], part[:], ALU.add).then_inc(sums_ready, 1)
                dve.wait_ge(sums_ready, t + 3)
                for u in range(2):
                    dve.wait_ge(rstd_ready, t * 4 + (2 * u + 4))
                    for k in range(KD):
                        normalise(u, k)
                        if k:
                            cross(u, k - 1)
                        if u == 0 and k in (2, 4):
                            invert(1, (k - 2) // 2)
                    cross(u, KD - 1)

            links = [0]

            def link(ins):
                ins.then_inc(dve_chain, 1)
                links[0] += 1
                dve.wait_ge(dve_chain, links[0])

            half = NMOD // 2

            def take(turned, bank, rows, first, last):
                dve.wait_ge(mod_ready, turned)
                columns = bank[:, 0:NCOL * rows].rearrange("p (c i b n) -> p i n b c", c=NCOL, b=D // BLOCK, n=NB)
                for i in range(first, last):
                    ins = v.tensor_copy(mod[:, i].rearrange("p n (b c) -> p n b c", c=NCOL), columns[:, i - first])
                link(ins)

            def gate(j):
                link(v.tensor_scalar(gate_t[:, j], mod[:, half * j + 2], 0.0, 2.0, ALU.is_ge, ALU.mult))
                link(v.tensor_scalar(gate_t[:, j], gate_t[:, j], -1.0, None, ALU.add))
                link(v.tensor_tensor(gate_a[:, j], mod[:, half * j + 2], gate_t[:, j], ALU.mult))
                link(v.scalar_tensor_tensor(gate_a[:, j], gate_a[:, j], GATE_MIN, gate_t[:, j], ALU.max, ALU.mult))

            take(2, ps_mod[0], ROWS[0] + ROWS[1], 0, half)
            v.tensor_scalar(ca1[:], mod[:, 1], 1.0, None, ALU.add)
            gate(0)

            dve.wait_ge(sqsum_done, (NPAIR + 2) * 2 * KD)
            dve.wait_ge(cross_done, (NPAIR + 2) * KD)
            link(v.tensor_tensor(sums[:], sums[:], part[:], ALU.add))
            link(v.tensor_tensor(xs[:], sums[:, 0], sums[:, 1], ALU.add))
            sa = mod[:, 0]
            w0, w1, w2, w3, w4 = (t_[:] for t_ in tmp)
            v.tensor_tensor(w0, ca1[:], xs[:, 2:4], ALU.mult)
            v.tensor_tensor(w1, sa, xs[:, 0:2], ALU.mult)
            v.tensor_tensor(w2, sa, sa, ALU.mult)
            v.tensor_tensor(w3[:, 0], ca1[:, 1], xs[:, 4], ALU.mult)
            link(v.tensor_tensor(w3[:, 1], ca1[:, 1], xs[:, 1], ALU.mult))
            v.scalar_tensor_tensor(w0, w1, 2.0, w0, ALU.mult, ALU.add)
            v.tensor_tensor(w4[:, 0], sa[:, 1], xs[:, 0], ALU.mult)
            link(v.tensor_scalar(w4[:, 1], sa[:, 1], float(C), None, ALU.mult))
            v.tensor_tensor(w0, w0, ca1[:], ALU.mult)
            link(v.tensor_tensor(w3, w3, w4, ALU.add))
            v.scalar_tensor_tensor(score[:, 0, 0], w2[:, 0], float(C), w0[:, 0], ALU.mult, ALU.add)
            v.scalar_tensor_tensor(score[:, 1, 1], w2[:, 1], float(C), w0[:, 1], ALU.mult, ALU.add)
            v.tensor_tensor(w4[:, 0], w3[:, 0], ca1[:, 0], ALU.mult)
            link(v.tensor_tensor(w4[:, 1], w3[:, 1], sa[:, 0], ALU.mult))
            v.tensor_tensor(score[:, 0, 1], w4[:, 0], w4[:, 1], ALU.add)
            link(v.tensor_tensor(score[:, 1, 0], w4[:, 0], w4[:, 1], ALU.add))
            link(v.tensor_tensor(w0, score[:, :, 0], score[:, :, 1], ALU.max))
            for m in range(NB):
                ins = v.tensor_tensor(score[:, :, m], score[:, :, m], w0, ALU.subtract)
            link(ins)
            v.tensor_scalar(score[:], score[:], SCORE_SCALE, None, ALU.mult).then_inc(shifted, 1)
            dve.wait_ge(exp_done, 1)
            link(v.tensor_tensor(w0, prob[:, :, 0], prob[:, :, 1], ALU.add))
            link(v.reciprocal(w1, w0))
            for m in range(NB):
                ins = v.tensor_tensor(prob[:, :, m], prob[:, :, m], w1, ALU.mult)
            link(ins)
            ga = gate_a[:, 0]
            for n in range(NB):
                v.scalar_tensor_tensor(att[:, n, n], prob[:, n, n], 1.0, ga[:, n], ALU.add, ALU.mult)
                ins = v.tensor_tensor(att[:, n, 1 - n], prob[:, n, 1 - n], ga[:, n], ALU.mult)
            link(ins)
            for n in range(NB):
                v.tensor_tensor(coef[:, 0, n], att[:, n, n], ca1[:, n], ALU.mult)
                v.tensor_tensor(coef[:, 1, n], att[:, n, 1 - n], ca1[:, 1 - n], ALU.mult)
                v.tensor_tensor(w2[:, n], att[:, n, n], sa[:, n], ALU.mult)
                ins = v.tensor_tensor(w3[:, n], att[:, n, 1 - n], sa[:, 1 - n], ALU.mult)
            link(ins)
            v.tensor_tensor(coef[:, 2], w2, w3, ALU.add).then_inc(coef_ready, 1)
            dve.wait_ge(coef_ready, 1)

            def split_lo(p, ahead, e):
                _, _, size = kind_of(p % NSLOT)
                r = p % 2
                dve.wait_ge(hi_ready, e * NSLOT + ahead + (p + 1))
                v.tensor_tensor(w_lo[r][:, 0:size], w_raw[r][:, 0:size], w_hi[r][:, 0:size].bitcast(F32),
                                ALU.subtract).then_inc(lo_ready, 1)

            for k in range(KD):
                dve.wait_ge(u0_ready, k + 1)
                for n in range(NB):
                    ins = v.scalar_tensor_tensor(u_0[:, k, n, :], xhat_0[:, k, 1 - n, :], coef[:, 1, n, k:k + 1],
                                                 u_0[:, k, n, :], ALU.mult, ALU.add)
                if k < X2_POOL:
                    ins.then_inc(v20_ready, 1)
                else:
                    link(ins)
                    v.tensor_tensor(acc[:, k], u_0[:, k], x_0[:, k], ALU.add).then_inc(x20_ready, 1)
            dve.wait_ge(x20_ready, KD - X2_POOL)
            v.nop().then_inc(next_free, 1)
            split_lo(0, 0, 0)
            dve.wait_ge(mean20_mm, 1)
            for j in range(NSQ):
                ks = slice(j * SQ_PER, (j + 1) * SQ_PER)
                v.scalar_tensor_tensor(tok(d_0)[:, ks], bc(ps_mean2, SQ_PER), -1.0 / D, tok(acc)[:, ks], ALU.mult,
                                       ALU.add).then_inc(d20_ready, 1)
            dve.wait_ge(d20_ready, NSQ)
            take(3, ps_mod[1], ROWS[2], half, half + 2)
            link(v.tensor_scalar(cb1[:], mod[:, half + 1], 1.0, None, ALU.add))
            for k in range(KD):
                for n in range(NB):
                    ins = v.tensor_scalar(u_0[:, k, n, :], d_0[:, k, n, :], cb1[:, n, k:k + 1], None, ALU.mult)
            link(ins)
            dve.sem_inc(gu_bank_free, 2)
            dve.wait_ge(std20_ready, 1)
            link(v.reciprocal(rstd2, std2))

            def low(k):
                dve.wait_ge(xn_hi_ready, k + 1)
                for n in range(NB):
                    cols = slice(n * CC, (n + 1) * CC)
                    ins = v.scalar_tensor_tensor(xn_lo[:, k, cols], u_0[:, k, n, :], mod[:, 3, n, k:k + 1],
                                                 xn_hi[:, k, cols].bitcast(F32), ALU.add, ALU.subtract)
                ins.then_inc(xn_ready, 1)

            for k in range(KD):
                v.tensor_tensor(tok(u_0)[:, k, :], tok(u_0)[:, k, :], rstd2, ALU.mult).then_inc(t20_ready, 1)
                if k:
                    low(k - 1)
            low(KD - 1)

            take(4, ps_mod[2], ROWS[3], half + 2, 2 * half)
            gate(1)

            dve.sem_inc(y_bank_free, 2)
            dve.sem_inc(h_ready, 1)
            dve.sem_inc(acc_ready, KD)

            split_lo(1, 0, 0)

            def chunk(e, last):
                def one(p, ahead):
                    kind, n, _ = kind_of(p)
                    if kind == "gu":
                        i = n if n < HALF0 else n - HALF0
                        tile = bass.ds(ahead + i, 1)
                        dve.wait_ge(silu_done, e * NGU + ahead + (n + 1))
                        dve.wait_ge(h_ready, e * NGU + ahead + (n + 1))
                        v.tensor_tensor(prod[:], ps_up[n % 2], sg[n % 2][:], ALU.mult).then_inc(gu_bank_free, 1)
                        dve.wait_ge(gu_bank_free, e * NGU + ahead + (n + 3))
                        v.tensor_scalar(h_hi[:, tile, :].rearrange("p o t -> p (o t)"), prod[:], 1.0, None,
                                        ALU.mult).then_inc(h_hi_done, 1)
                        dve.wait_ge(h_hi_done, e * NGU + ahead + (n + 1))
                        v.tensor_tensor(h_lo[:, tile, :].rearrange("p o t -> p (o t)"), prod[:],
                                        h_hi[:, tile, :].rearrange("p o t -> p (o t)").bitcast(F32),
                                        ALU.subtract).then_inc(h_ready, 1)
                    elif kind == "tail":
                        dve.wait_ge(silu_done, e * NGU + (n + 1))
                        dve.wait_ge(h_ready, e * NGU + (n + 1))
                        v.tensor_tensor(prod[0:TAIL, :], ps_gate[n % 2][TAIL:P, :], sg[n % 2][0:TAIL, :],
                                        ALU.mult).then_inc(gu_bank_free, 1)
                        dve.wait_ge(gu_bank_free, e * NGU + (n + 3))
                        v.tensor_scalar(h_hi[0:TAIL, HT - 1, :], prod[0:TAIL, :], 1.0, None, ALU.mult).then_inc(h_hi_done, 1)
                        dve.wait_ge(h_hi_done, e * NGU + (n + 1))
                        v.tensor_tensor(h_hi[TAIL:P, HT - 1, :], prod[0:TAIL, :], h_hi[0:TAIL, HT - 1, :].bitcast(F32),
                                        ALU.subtract).then_inc(h_ready, 1)
                    else:
                        m = n % KD
                        if n < KD:
                            dve.wait_ge(acc_ready, e * KD + KD)
                        dve.wait_ge(slot_done, e * NSLOT + ahead + (p + 1))
                        for b in range(NB):
                            tile = acc[:, bass.ds(ahead + m, 1), b, :].rearrange("p o c -> p (o c)")
                            ins = v.scalar_tensor_tensor(tile, ps_y[n % 2][:, b * CC:(b + 1) * CC],
                                                         gate_a[:, 1, b, bass.ds(ahead + m, 1)], tile, ALU.mult, ALU.add)
                        ins.then_inc(y_bank_free, 1)
                    if not (last and p + 2 >= NSLOT):
                        split_lo(p + 2, ahead, e)
                    for sums_split, at_step in enumerate((P_GU1 - 2, P_TAIL - 2)):
                        if p == at_step and not last:
                            dve.wait_ge(sum_hi_ready, e * 2 + (sums_split + 1))
                            v.tensor_tensor(sum_lo[:], pool_acc, sum_hi[:].bitcast(F32), ALU.subtract).then_inc(sum_lo_ready, 1)
                    if p == P_TAIL - 1 and not last:
                        dve.wait_ge(std2_ready, e + 1)
                        v.reciprocal(rstd2, std2).then_inc(rstd2_ready, 1)
                    if p == NSLOT - 3 and not last:
                        for k in range(KD):
                            dve.wait_ge(xn_hi_ready, e * KD + (KD + k + 1))
                            v.tensor_tensor(xn_lo[:, k, :], tok(h_next)[:, k, :], xn_hi[:, k, :].bitcast(F32),
                                            ALU.subtract).then_inc(xn_ready, 1)
                steps(dve, one)

            with dve.Fori(0, NCH - 1) as e:
                chunk(e, False)
            chunk(NCH - 1, True)

        @block.tensor
        def _(pe):
            mm = nc.tensor.matmul
            pe.sem_inc(mean_mm, 4)
            pe.sem_inc(sq_pair_used, 2)
            pe.wait_ge(ones_ready, 1)

            def modulate(r, bank, j, group):
                rows, block, cols = ROWS[group], j // 2, slice(j % 2 * WPART, (j % 2 + 1) * WPART)
                start = max(ROWS) - NB - block * NB
                for k in range(KD):
                    ins = mm(bank[0:rows, cols], silu_pad[:, k, start:start + rows], wm[r][:, k, :],
                             start=j == k == 0, stop=j == GROUP[group] - 1 and k == KD - 1)
                ins.then_inc(mod_done, 1)

            def turn(group, bank, rows, at):
                pe.wait_ge(rows_copied, group + 1)
                n = ROWS[group]
                for c in range(NCOL):
                    ins = mm(bank[:, c * rows + at:c * rows + at + n], mod_rows[group][0:n, c * P:(c + 1) * P],
                             eye_t[0:n, 0:n], start=True, stop=True)
                ins.then_inc(mod_ready, 1)

            def parts(group, js):
                for j in js:
                    w = FIRST[group] + j
                    pe.wait_ge(wm_loaded[w % WM_RING], 16 * (w // WM_RING) + 16)
                    modulate(w % WM_RING, ps_rows[group], j, group)

            for t in range(NPAIR // 2):
                def means(u, h):
                    i = 2 * u + h
                    pe.wait_ge(x_loaded[u][h], t * 16 + 16)
                    pe.wait_ge(mean_ready, t * 4 + (i + 1))
                    for k in range(PRE[t], KD):
                        mm(ps_mean[u][h], ones[:], tok(xbuf[u][:, h])[:, k, :], start=k == PRE[t], stop=False)
                    pe.wait_ge(presum_ready, t * 4 + (i + 1))
                    mm(ps_mean[u][h], ones[:], presums[u][:, h, :], start=PRE[t] == KD, stop=True).then_inc(mean_mm, 1)

                def variances(u, h):
                    i = 2 * u + h
                    pe.wait_ge(std_ready, t * 4 + (i + 1))
                    for j in range(NSQ):
                        pe.wait_ge(sq_added, t * (4 * NSQ) + (i * NSQ + j + 3))
                        mm(ps_var[h], ones[:], sq_pair[:, j % 2, :], start=j == 0, stop=j == NSQ - 1).then_inc(sq_pair_used, 1)

                if t == 0:
                    means(0, 0)
                    means(0, 1)
                    means(1, 0)
                    variances(0, 0)
                    means(1, 1)
                    variances(0, 1)
                    pe.wait_ge(silu_ready, 1)
                    parts(0, range(2))
                    variances(1, 0)
                    variances(1, 1)
                    parts(0, range(2, GROUP[0]))
                else:
                    means(0, 0)
                    means(0, 1)
                    means(1, 0)
                    means(1, 1)
                    parts(1, range(2))
                    variances(0, 0)
                    variances(0, 1)
                    parts(1, range(2, 4))
                    variances(1, 0)
                    variances(1, 1)
                    parts(1, range(4, GROUP[1]))

            pe.wait_ge(eye_loaded, 16)
            pe.wait_ge(mean_ready, NCH + 4)
            parts(2, range(4))
            turn(0, ps_mod[0], ROWS[0] + ROWS[1], 0)
            turn(1, ps_mod[0], ROWS[0] + ROWS[1], ROWS[0])
            parts(2, range(4, GROUP[2]))
            parts(3, range(1))

            for k in range(KD):
                if k < X2_POOL:
                    pe.wait_ge(x20_pool, k + 1)
                else:
                    pe.wait_ge(x20_ready, k - X2_POOL + 1)
                ins = mm(ps_mean2, ones[:], tok(acc)[:, k, :], start=k == 0, stop=k == KD - 1)
            ins.then_inc(mean20_mm, 1)
            turn(2, ps_mod[1], ROWS[2], 0)
            parts(3, range(1, 2))
            for j in range(NSQ):
                pe.wait_ge(sq20_ready, j + 1)
                for k in range(SQ_PER):
                    ins = mm(ps_var2, ones[:], sq[:, j % 2, k, :], start=j == k == 0, stop=j == NSQ - 1 and k == SQ_PER - 1)
                ins.then_inc(sq20_used, 1)
            parts(3, range(2, GROUP[3]))
            turn(3, ps_mod[2], ROWS[3], 0)

            def gate_up(p, ahead, e):
                kind, n, _ = kind_of(p)
                r = p % 2
                pe.wait_ge(lo_ready, e * NSLOT + ahead + (p + 1))
                pe.wait_ge(gu_bank_free, e * NGU + ahead + (n + 1))
                banks = (ps_gate[n % 2], ps_up[n % 2]) if kind == "gu" else (ps_gate[n % 2],)
                order = [(j, k) for j in range(len(banks)) for k in range(KD)]
                if p == 0:
                    order.sort(key=lambda jk: jk[1])
                for j, k in order:
                    w = slice((j * KD + k) * P, (j * KD + k + 1) * P)
                    if p == 0 and j == 0:
                        pe.wait_ge(xn_ready, e * KD + (k + 1))
                    mm(banks[j], w_hi[r][:, w], xn_hi[:, k, :], start=k == 0, stop=False)
                    mm(banks[j], w_hi[r][:, w], xn_lo[:, k, :], start=False, stop=False)
                    ins = mm(banks[j], w_lo[r][:, w], xn_hi[:, k, :], start=False, stop=k == KD - 1)
                ins.then_inc(slot_done, 1)

            def down(p, ahead, e):
                _, n, _ = kind_of(p)
                half = n // KD
                r = p % 2
                bank = ps_y[n % 2]
                pe.wait_ge(lo_ready, e * NSLOT + ahead + (p + 1))
                pe.wait_ge(y_bank_free, e * NDN + ahead + (n + 1))
                known = HALF0 if half == 0 else NGU
                pe.wait_ge(h_ready, e * NGU + known)
                for k in range(HT):
                    w = slice(k * P, (k + 1) * P)
                    if k == HT - 1:
                        pe.wait_ge(h_ready, e * NGU + (known + 1))
                    if half == 1 and k == HT - 1:
                        mm(bank, w_hi[r][:, w], h_hi[:, k, :], start=False, stop=False)
                        ins = mm(bank, w_lo[r][:, w], h_hi[:, k, :], start=False, stop=True)
                    else:
                        mm(bank, w_hi[r][:, w], h_hi[:, k, :], start=k == 0, stop=False)
                        mm(bank, w_hi[r][:, w], h_lo[:, k, :], start=False, stop=False)
                        ins = mm(bank, w_lo[r][:, w], h_hi[:, k, :], start=False, stop=k == HT - 1)
                ins.then_inc(slot_done, 1)

            def loop(slot, first, n, e):
                with pe.Fori(0, n // 2) as i:
                    for u in range(2):
                        slot(first + u, 2 * i, e)
                if n % 2:
                    slot(first + n - 1, 0, e)

            def sum_over_features(bank, count):
                pe.wait_ge(sum_lo_ready, count)
                mm(bank, ones_r[:], sum_hi[:], start=True, stop=False)
                mm(bank, ones_r[:], sum_lo[:], start=False, stop=True).then_inc(stat2_mm, 1)

            pe.wait_ge(ones_r_ready, 1)

            def chunk(e, last):
                gate_up(0, 0, e)
                loop(gate_up, 1, HALF0 - 1, e)
                loop(down, P_DN0, KD, e)
                if not last:
                    sum_over_features(ps_mean2, e * 2 + 1)
                loop(gate_up, P_GU1, HALF1, e)
                if not last:
                    sum_over_features(ps_var2, e * 2 + 2)
                gate_up(P_TAIL, 0, e)
                loop(down, P_DN1, KD, e)

            with pe.Fori(0, NCH - 1) as e:
                chunk(e, False)
            chunk(NCH - 1, True)


def chunks_of(a):
    return np.ascontiguousarray(a.reshape(NB, NCH, CC, KD, P).transpose(1, 4, 3, 0, 2)).reshape(NCH, P, KD * T)


def tiles_of(w, n):
    return w.reshape(n, KD, P).transpose(2, 1, 0)


def kernel(L0_attn_x, L0_ffn_W_gate, L0_ffn_W_up, L0_ffn_W_down, L0_c, L0_wmod):
    import concourse.bacc as bacc
    from concourse.bass_utils import run_bass_kernel_spmd

    xin, wg, wu, wd, c, wmod = (np.asarray(a) for a in (L0_attn_x, L0_ffn_W_gate, L0_ffn_W_up, L0_ffn_W_down, L0_c, L0_wmod))
    whole = FT * P
    gu = np.stack([np.stack([tiles_of(w[f * P:(f + 1) * P], P) for w in (wg, wu)], 1) for f in range(FT)])
    gut = np.concatenate([tiles_of(wg[whole:], TAIL), tiles_of(wu[whole:], TAIL)], 2)
    wdt = wd.T
    blocks = [wdt[f * P:(f + 1) * P] for f in range(FT)] + [np.concatenate([wdt[whole:], wdt[whole:]], 0)]
    halves = [np.stack(blocks[:HALF0]), np.stack(blocks[HALF0:])]
    dn = np.stack([h.reshape(HT, P, KD, P).transpose(2, 1, 0, 3) for h in halves])
    arrays = {
        "x": chunks_of(xin),
        "wgu": np.ascontiguousarray(gu).reshape(FT, P, GU),
        "wgut": np.ascontiguousarray(gut).reshape(1, P, GUT),
        "wdn": np.ascontiguousarray(dn).reshape(NDN, P, DN),
        "cT": np.ascontiguousarray(c.reshape(NB, KD, P).transpose(2, 1, 0)),
        "eye": np.eye(max(ROWS), dtype=np.float32),
        "wmod": np.ascontiguousarray(wmod.reshape(KD, P, NPART, WPART).transpose(2, 1, 0, 3)),
    }
    nc = bacc.Bacc("TRN2", target_bir_lowering=False, num_devices=1)
    args = [nc.dram_tensor(n, a.shape, mybir.dt.from_np(a.dtype), kind="ExternalInput").ap() for n, a in arrays.items()]
    out = nc.dram_tensor("out", (NCH, P, KD * T), F32, kind="ExternalOutput").ap()
    build(nc, *args, out)
    r = run_bass_kernel_spmd(nc, [arrays], core_ids=[0])
    y = r.results[0]["out"].reshape(NCH, P, KD, NB, CC)
    return np.ascontiguousarray(y.transpose(3, 0, 4, 2, 1)).reshape(NB, C, D)
```
